# Optimizing a Trainium2 kernel written in Bass

```python
import numpy as np
import jax
import jax.numpy as jnp

def _softmax(x, axis=-1):
    return jax.nn.softmax(x, axis=axis)

def _gelu(x):
    return jax.nn.gelu(x, approximate=True)

def _silu(x):
    return jax.nn.silu(x)

def _sigmoid(x):
    return jax.nn.sigmoid(x)

def _layernorm(x, axis=-1, eps=1e-05):
    m = jnp.mean(x, axis=axis, keepdims=True)
    v = jnp.var(x, axis=axis, keepdims=True)
    return (x - m) / jnp.sqrt(v + eps)

def _scatter_add(tgt, idx, src, axis=0):
    return tgt.at[idx].add(src)

def _segment_sum(src, seg, n):
    return jax.ops.segment_sum(src, seg, n)
kernel_name = 'mk_macaron_d2_jaxref_r4_25161d'

def setup_inputs(seed: int=0):
    np.random.seed(seed)
    _w = jnp.asarray

    def _L0_attn_setup():
        import jax, jax.numpy as jnp
        import numpy as np
        HIDDEN = 512
        KEY = 512
        EPS = 1e-05
        key = jax.random.key(seed)
        k1, k2, k3 = jax.random.split(key, 3)
        B, S = (4, 512)
        x = jax.random.normal(k1, (B, S, HIDDEN), dtype=jnp.float32)
        bq = 1.0 / np.sqrt(HIDDEN)
        qkv = jax.random.uniform(k2, (HIDDEN, KEY * 3), minval=-bq, maxval=bq, dtype=jnp.float32)
        bo = 1.0 / np.sqrt(KEY)
        o_proj = jax.random.uniform(k3, (KEY, HIDDEN), minval=-bo, maxval=bo, dtype=jnp.float32)
        gamma = jnp.ones((HIDDEN,), dtype=jnp.float32)
        beta = jnp.zeros((HIDDEN,), dtype=jnp.float32)
        return {'x': x, 'qkv': qkv, 'o_proj': o_proj, 'gamma': gamma, 'beta': beta}
    _L0_attn_in = _L0_attn_setup()

    def _L0_ffn_setup():
        import jax, jax.numpy as jnp
        import numpy as np
        B, S, D, H = (4, 512, 512, 2048)

        def fwht(x):
            orig_shape = x.shape
            n = orig_shape[-1]
            x = x.reshape(-1, n)
            h = 1
            while h < n:
                xb = x.reshape(-1, n // (2 * h), 2, h)
                a = xb[:, :, 0, :]
                b = xb[:, :, 1, :]
                x = jnp.stack([a + b, a - b], axis=2).reshape(-1, n)
                h *= 2
            scale = jnp.asarray(1.0 / np.sqrt(n), dtype=x.dtype)
            return (x * scale).reshape(orig_shape)
        key = jax.random.key(seed)
        kx, k1, k2, k3 = jax.random.split(key, 4)
        x = jax.random.normal(kx, (B, S, D), dtype=jnp.float32)
        W1 = jax.random.normal(k1, (H, D), dtype=jnp.float32) * (1.0 / np.sqrt(D))
        W2 = jax.random.normal(k2, (D, H), dtype=jnp.float32) * (1.0 / np.sqrt(H))
        W3 = jax.random.normal(k3, (H, D), dtype=jnp.float32) * (1.0 / np.sqrt(D))
        return {'x': x, 'W1': W1, 'W2': W2, 'W3': W3}
    _L0_ffn_in = _L0_ffn_setup()

    def _L1_attn_setup():
        import jax, jax.numpy as jnp
        import numpy as np
        BATCH, SEQ, D_MODEL, D_STATE = (4, 1024, 512, 256)
        key = jax.random.key(seed)
        kx, kb, kc = jax.random.split(key, 3)
        x = jax.random.normal(kx, (BATCH, SEQ, D_MODEL), dtype=jnp.float32)
        B = jax.random.normal(kb, (D_STATE, D_MODEL), dtype=jnp.float32) * 0.01
        C = jax.random.normal(kc, (D_MODEL, D_STATE), dtype=jnp.float32) * 0.01
        D = jnp.zeros((D_MODEL,), dtype=jnp.float32)
        return {'x': x, 'B': B, 'C': C, 'D': D}
    _L1_attn_in = _L1_attn_setup()

    def _L1_ffn_setup():
        import jax, jax.numpy as jnp
        import numpy as np
        HIDDEN = 512
        INTER = 1408
        B, S = (2, 512)

        def _ternary(key, shape):
            return jax.random.randint(key, shape, -1, 2).astype(jnp.float32)
        key = jax.random.key(seed)
        ks = jax.random.split(key, 7)
        x = jax.random.normal(ks[0], (B, S, HIDDEN), dtype=jnp.float32)
        gate_w = _ternary(ks[1], (INTER, HIDDEN))
        up_w = _ternary(ks[2], (INTER, HIDDEN))
        down_w = _ternary(ks[3], (HIDDEN, INTER))
        gate_s = jax.random.uniform(ks[4], (INTER,), minval=0.01, maxval=0.1, dtype=jnp.float32)
        up_s = jax.random.uniform(ks[5], (INTER,), minval=0.01, maxval=0.1, dtype=jnp.float32)
        down_s = jax.random.uniform(ks[6], (HIDDEN,), minval=0.01, maxval=0.1, dtype=jnp.float32)
        return {'x': x, 'gate_w': gate_w, 'up_w': up_w, 'down_w': down_w, 'gate_s': gate_s, 'up_s': up_s, 'down_s': down_s}
    _L1_ffn_in = _L1_ffn_setup()
    _d = {'L0_attn_x': _L0_attn_in['x'], 'L0_attn_qkv': _L0_attn_in['qkv'], 'L0_attn_o_proj': _L0_attn_in['o_proj'], 'L0_attn_gamma': _L0_attn_in['gamma'], 'L0_attn_beta': _L0_attn_in['beta'], 'L0_ffn_W1': _L0_ffn_in['W1'], 'L0_ffn_W2': _L0_ffn_in['W2'], 'L0_ffn_W3': _L0_ffn_in['W3'], 'L1_attn_B': _L1_attn_in['B'], 'L1_attn_C': _L1_attn_in['C'], 'L1_attn_D': _L1_attn_in['D'], 'L1_ffn_gate_w': _L1_ffn_in['gate_w'], 'L1_ffn_up_w': _L1_ffn_in['up_w'], 'L1_ffn_down_w': _L1_ffn_in['down_w'], 'L1_ffn_gate_s': _L1_ffn_in['gate_s'], 'L1_ffn_up_s': _L1_ffn_in['up_s'], 'L1_ffn_down_s': _L1_ffn_in['down_s']}
    _x0 = _d['L0_attn_x']
    _d['L0_attn_x'] = jax.random.normal(jax.random.fold_in(jax.random.key(seed), 1), (4, 512, 512), dtype=_x0.dtype)
    del _x0
    return _d

def reference(L0_attn_x, L0_attn_qkv, L0_attn_o_proj, L0_attn_gamma, L0_attn_beta, L0_ffn_W1, L0_ffn_W2, L0_ffn_W3, L1_attn_B, L1_attn_C, L1_attn_D, L1_ffn_gate_w, L1_ffn_up_w, L1_ffn_down_w, L1_ffn_gate_s, L1_ffn_up_s, L1_ffn_down_s):

    def _L0_attn_ref(x, qkv, o_proj, gamma, beta):
        import jax, jax.numpy as jnp
        import numpy as np
        HIDDEN = 512
        KEY = 512
        EPS = 1e-05
        residual = x
        mu = jnp.mean(x, axis=-1, keepdims=True)
        var = jnp.mean((x - mu) ** 2, axis=-1, keepdims=True)
        x_norm = (x - mu) / jnp.sqrt(var + EPS) * gamma + beta
        q = x_norm @ qkv[:, :KEY]
        k = x_norm @ qkv[:, KEY:2 * KEY]
        v = x_norm @ qkv[:, 2 * KEY:]
        scale = 1.0 / jnp.sqrt(jnp.float32(KEY))
        scores = jnp.einsum('bsk,btk->bst', q, k) * scale
        S_len = x.shape[1]
        causal = jnp.tril(jnp.ones((S_len, S_len), dtype=bool))
        scores = jnp.where(causal[None], scores, -jnp.inf)
        attn = jax.nn.softmax(scores, axis=-1)
        out = attn @ v
        out = out @ o_proj
        return out + residual

    def _L0_ffn_ref(x, W1, W2, W3):
        import jax, jax.numpy as jnp
        import numpy as np
        B, S, D, H = (4, 512, 512, 2048)

        def fwht(x):
            orig_shape = x.shape
            n = orig_shape[-1]
            x = x.reshape(-1, n)
            h = 1
            while h < n:
                xb = x.reshape(-1, n // (2 * h), 2, h)
                a = xb[:, :, 0, :]
                b = xb[:, :, 1, :]
                x = jnp.stack([a + b, a - b], axis=2).reshape(-1, n)
                h *= 2
            scale = jnp.asarray(1.0 / np.sqrt(n), dtype=x.dtype)
            return (x * scale).reshape(orig_shape)
        up_gate = jnp.einsum('bsd,hd->bsh', x, W1)
        up_lin = jnp.einsum('bsd,hd->bsh', x, W3)
        hidden = jax.nn.silu(up_gate) * up_lin
        hidden = fwht(hidden)
        out = jnp.einsum('bsh,dh->bsd', hidden, W2)
        return out

    def _L1_attn_ref(x, B, C, D):
        import jax, jax.numpy as jnp
        import numpy as np
        BATCH, SEQ, D_MODEL, D_STATE = (4, 1024, 512, 256)
        state = jnp.tanh(jnp.einsum('bsd,nd->bsn', x, B))
        return jnp.einsum('bsn,dn->bsd', state, C) + D * x

    def _L1_ffn_ref(x, gate_w, up_w, down_w, gate_s, up_s, down_s):
        import jax, jax.numpy as jnp
        import numpy as np
        HIDDEN = 512
        INTER = 1408
        B, S = (2, 512)

        def _ternary(key, shape):
            return jax.random.randint(key, shape, -1, 2).astype(jnp.float32)
        b, s, h = x.shape
        xf = x.reshape(b * s, h)
        g = jnp.einsum('th,ih->ti', xf, gate_w) * gate_s
        u = jnp.einsum('th,ih->ti', xf, up_w) * up_s
        hdn = jax.nn.silu(g) * u
        out = jnp.einsum('ti,hi->th', hdn, down_w) * down_s
        return out.reshape(b, s, -1)
    x = L0_attn_x
    x = x + 0.5 * _L0_ffn_ref(_layernorm(x, axis=-1), L0_ffn_W1, L0_ffn_W2, L0_ffn_W3)
    x = x + _L0_attn_ref(_layernorm(x, axis=-1), L0_attn_qkv, L0_attn_o_proj, L0_attn_gamma, L0_attn_beta)
    x = x + 0.5 * _L0_ffn_ref(_layernorm(x, axis=-1), L0_ffn_W1, L0_ffn_W2, L0_ffn_W3)
    x = x + 0.5 * _L1_ffn_ref(_layernorm(x, axis=-1), L1_ffn_gate_w, L1_ffn_up_w, L1_ffn_down_w, L1_ffn_gate_s, L1_ffn_up_s, L1_ffn_down_s)
    x = x + _L1_attn_ref(_layernorm(x, axis=-1), L1_attn_B, L1_attn_C, L1_attn_D)
    x = x + 0.5 * _L1_ffn_ref(_layernorm(x, axis=-1), L1_ffn_gate_w, L1_ffn_up_w, L1_ffn_down_w, L1_ffn_gate_s, L1_ffn_up_s, L1_ffn_down_s)
    return x

_drawn_inputs = setup_inputs


def setup_inputs(seed=0):
    import zlib

    import numpy as np

    out = dict(_drawn_inputs(seed))
    spreads = {'L0_attn_gamma': (1.0, 0.6), 'L0_attn_beta': (0.0, 0.481), 'L1_attn_D': (0.0, 0.1)}
    factors = {'L1_attn_B': 3.95, 'L1_attn_C': 3.934}
    for name, (base, spread) in spreads.items():
        noise = np.random.default_rng([zlib.crc32(name.encode()), seed]).standard_normal(out[name].shape)
        drawn = base * np.exp(spread * noise) if base else spread * noise
        out[name] = jnp.asarray(drawn.astype(out[name].dtype))
    for name, factor in factors.items():
        out[name] = (out[name] * factor).astype(out[name].dtype)
    return out
```

```python
from contextlib import ExitStack

import numpy as np

import concourse.bass as bass
import concourse.mybir as mybir
from concourse.alu_op_type import AluOpType as ALU

F32 = mybir.dt.float32
F32R = mybir.dt.float32r
ACT = mybir.ActivationFunctionType
AX = mybir.AxisListType

P = 128
D = 512
KD = D // P
CH = 4
TOK = 512
TT = TOK // P
HA = 2048
HB = 1408
HS = 256
EPS = 1e-5
SCORE_SCALE = D ** -0.5
MASKED = -3e38

SIZES = {"A": [2] * (HA // 256), "B": [2, 2, 2, 2, 1, 2], "S": [2], "T": []}
LAYERS = ["A", "T", "A", "B", "S", "B"]
LAST = len(LAYERS) - 1
assert sum(SIZES["A"]) * P == HA and sum(SIZES["B"]) * P == HB and sum(SIZES["S"]) * P == HS


class Plan:

    def __init__(self):
        self.use, self.block, self.tile, self.parts = {}, {}, {}, {}
        self.after = {}
        use = block = tile = parts = 0
        for c in (0, 1):
            for half in (0, 1):
                self.use["x", 0, c, half] = use
                use += 1
        for li, kind in enumerate(LAYERS):
            if kind == "T":
                for j in (0, 1):
                    self.use["q", 0, j] = use
                    use += 1
                for c in range(CH):
                    self.tile[li, c] = tile
                    tile += TT
                    for key in attention_uses(c):
                        self.use[key] = use
                        use += 1
                continue
            sizes = SIZES[kind]
            for g, size in enumerate(sizes):
                parts += 2 if kind == "S" else 3
                self.parts[li, g] = parts
                for c in range(CH):
                    self.tile[li, g, c] = tile
                    tile += TT
                    for b in range(size):
                        self.use[li, g, c, b] = use
                        self.block[li, g, c, b] = block
                        use, block = use + 1, block + 1
                        key = None
                        if g == 0 and c in (0, 1) and not (c == 0 and li and LAYERS[li - 1] == "T"):
                            key = ("x", li, c + 2, b)
                        if g == len(sizes) - 1 and c in (2, 3) and li < LAST:
                            key = ("x", li + 1, c - 2, b)
                        if key:
                            self.after[li, g, c, b] = key
                            self.use[key] = use
                            use += 1
        self.tiles = tile


def attention_uses(c):
    first = ("x", 1, c + 2) if c < 2 else ("x", 2, c - 1)
    keys = [("v", c, 0), ("p", c, 0), ("v", c, 1), first + (0,), ("p", c, 1)]
    keys += [("q", c + 1, 0)] if c + 1 < CH else []
    keys += [("p", c, 2), first + (1,)]
    keys += [("q", c + 1, 1)] if c + 1 < CH else []
    keys += [("p", c, 3)]
    keys += [("x", 2, 0, 0), ("x", 2, 0, 1)] if c == 1 else []
    return keys


def previous(li, g):
    if g:
        return li, g - 1
    if li == 0 or LAYERS[li - 1] == "T":
        return None
    return li - 1, len(SIZES[LAYERS[li - 1]]) - 1


def following(li, g):
    if g + 1 < len(SIZES[LAYERS[li]]):
        return li, g + 1
    if li == LAST or LAYERS[li + 1] == "T":
        return None
    return li + 1, 0


def group_buffer(li, g):
    return (sum(len(SIZES[k]) for k in LAYERS[:li]) + g) % 2


def build(nc, t):
    plan = Plan()
    use, block_no, tile_no, parts_no = plan.use, plan.block, plan.tile, plan.parts

    w2_scratch = nc.dram_tensor("w2_scratch", [HA // P, P, D], F32).ap()

    with ExitStack() as ctx:
        def sb(name, shape, dt=F32):
            return ctx.enter_context(nc.sbuf_tensor(name, shape, dt))

        def sem(name):
            return ctx.enter_context(nc.semaphore(name))

        mix_at = -(-nc.sbuf_base // 64) * 64
        mix_hi = sb("mix_hi", [P, 2, KD, D], F32R)
        mix_lo = sb("mix_lo", [P, 2, KD, D], F32R)
        x = sb("x", [P, CH * TT, D])
        xT_hi = sb("xT_hi", [P, CH, KD, TOK], F32R)
        xT_lo = sb("xT_lo", [P, CH, KD, TOK], F32R)
        raw = sb("raw", [P, 3, 2 * D])
        w_hi = [sb(f"w_hi{i}", [P, 3, 2 * D], F32R) for i in range(2)]
        w_lo = [sb(f"w_lo{i}", [P, 3, 2 * D], F32R) for i in range(2)]
        hid = [sb(f"hid{i}", [P, TOK]) for i in range(2)]
        hid_hi = [sb(f"hid_hi{i}", [P, TOK], F32R) for i in range(2)]
        hid_lo = [sb(f"hid_lo{i}", [P, TOK], F32R) for i in range(2)]
        xn = [sb(f"xn{i}", [P, D]) for i in range(2)]
        ident = sb("ident", [P, P])
        causal = sb("causal", [P, P])
        half_down_s = sb("half_down_s", [P, D])
        skip_d = nc.alloc_sbuf_tensor_at("skip_d", [P, D], F32, offset=mix_at)
        skip_t = nc.alloc_sbuf_tensor_at("skip_t", [P, D], F32, offset=mix_at + 4 * D)[:, :]
        small = sb("small", [P, 2 * KD + 2 * (HB // P)])
        gamma, beta = small[:, 0:KD], small[:, KD:2 * KD]
        gate_s = small[:, 2 * KD:2 * KD + HB // P]
        up_s = small[:, 2 * KD + HB // P:]
        stats = sb("stats", [P, TT, 6])
        meanvar = sb("meanvar", [P, CH * TT, 2])
        rstd = sb("rstd", [P, CH * TT])
        stats2 = sb("stats2", [P, 2, 6])
        meanvar2 = sb("meanvar2", [P, 2, 2])
        rstd2 = sb("rstd2", [P, 2])
        var_eps = sb("var_eps", [P, TT])
        minus_half = sb("minus_half", [P, TT])
        rowmax = sb("rowmax", [P, TT])
        negmax = sb("negmax", [P, TT])
        rowsum = sb("rowsum", [P, TT])
        rowinv = sb("rowinv", [P, TT])

        qT_hi = w_hi[0][:, 0:2, :].rearrange("p a (k t) -> p (a k) t", k=2)
        qT_lo = w_lo[0][:, 0:2, :].rearrange("p a (k t) -> p (a k) t", k=2)
        v_hi = w_hi[1][:, 0:2, :].rearrange("p a (k t) -> p (a k) t", k=2)
        v_lo = w_lo[1][:, 0:2, :].rearrange("p a (k t) -> p (a k) t", k=2)

        work = ctx.enter_context(nc.psum_tensor("work", [P, 4, D], F32))
        acc = ctx.enter_context(nc.psum_tensor("acc", [P, 4, D], F32))

        consts_in = sem("consts_in")
        x_in = [sem(f"x_in{c}") for c in range(CH)]
        raw_in = sem("raw_in")
        pair_full = sem("pair_full")
        pair_free = sem("pair_free")
        act_ready = sem("act_ready")
        hid_hi_ready = sem("hid_hi_ready")
        hid_lo_ready = sem("hid_lo_ready")
        acc_ready = sem("acc_ready")
        acc_free = sem("acc_free")
        w_hi_ready = sem("w_hi_ready")
        w_ready = sem("w_ready")
        w_scaled = sem("w_scaled")
        xn_ready = sem("xn_ready")
        xT_hi_ready = sem("xT_hi_ready")
        affine_ready = sem("affine_ready")
        stats_ready = sem("stats_ready")
        rstd_ready = sem("rstd_ready")
        stats2_ready = sem("stats2_ready")
        rstd2_ready = sem("rstd2_ready")
        att_hi_ready = sem("att_hi_ready")
        score_ready = sem("score_ready")
        max_ready = sem("max_ready")
        exp_ready = sem("exp_ready")
        dve_step = sem("dve_step")
        pool_step = sem("pool_step")
        skip_in = sem("skip_in")
        out_done = sem("out_done")
        fw_in = [sem(f"fw_in{i}") for i in range(4)]
        fw_taken = sem("fw_taken")
        had_ready = sem("had_ready")
        fw_hi_ready = sem("fw_hi_ready")
        fw_ready = sem("fw_ready")
        fw_full = sem("fw_full")
        fw_out = sem("fw_out")
        scratch_done = sem("scratch_done")
        fly_ready = sem("fly_ready")
        att_w_in = [sem(f"att_w_in{i}") for i in range(4)]
        att_w_hi = sem("att_w_hi")
        att_w_ready = sem("att_w_ready")
        mix_full = sem("mix_full")
        mix_hi_ready = sem("mix_hi_ready")
        mix_ready = sem("mix_ready")
        halt_x = sem("halt_x")

        SL = HA // P * P
        fw_buf = [x[:, 8:12, :], x[:, 12:16, :]]
        fw_tmp = x[:, 4:8, :]
        had = hid_hi[0][:, 0:P]
        neg_had = hid_hi[0][:, P:2 * P]
        att_raw = [x[:, 8:12, :], x[:, 12:16, :], x[:, 4:8, :], x[:, 8:12, :]]
        att_at = [1, 2, 3, 1]

        block = ctx.enter_context(nc.Block())

        def three(pe, out, a_hi, a_lo, b_hi, b_lo, start, stop):
            pe.matmul(out, a_hi, b_hi, start=start, stop=False)
            pe.matmul(out, a_hi, b_lo, start=False, stop=False)
            return pe.matmul(out, a_lo, b_hi, start=False, stop=stop)

        @block.sync
        def _(sp):
            sp.dma_start(ident[:, :], t["ident"]).then_inc(consts_in, 16)
            sp.dma_start(hid[0][:, 0:P], t["hadamard"]).then_inc(consts_in, 16)
            sp.dma_start(causal[:, :], t["causal"]).then_inc(consts_in, 16)
            sp.dma_start(small[:, :], t["small"]).then_inc(consts_in, 16)
            sp.dma_start(half_down_s[:, :], t["down_s"]).then_inc(consts_in, 16)
            sp.dma_start(x[:, 0:TT, :], t["x"][:, 0:TT, :]).then_inc(x_in[0], 16)
            for s in range(4):
                if s >= 2:
                    sp.wait_ge(fw_taken, s - 1)
                sp.dma_start(fw_buf[s % 2].rearrange("p a (b d) -> p (a b) d", b=4),
                             t["w2a"][s]).then_inc(fw_in[s], 16)

            def scratch(s):
                sp.wait_ge(fw_out, 4 * (s + 1))
                sp.dma_start(w2_scratch[:, :, s * P:(s + 1) * P].rearrange("b p d -> p b d"),
                             raw[:, 0:2, :].rearrange("p a (b d) -> p (a b) d", d=P)
                             ).then_inc(scratch_done, 16)

            scratch(0)
            scratch(1)
            for i in range(4):
                if i < 2:
                    sp.wait_ge(fw_taken, 3 + i)
                elif i == 2:
                    sp.wait_ge(fly_ready, 4)
                else:
                    sp.wait_ge(att_w_ready, 1)
                if i == 2:
                    scratch(2)
                sp.dma_start(att_raw[i], t["att_w"][i]).then_inc(att_w_in[i], 16)
            scratch(3)

            def load(src, b0, size, parts=(0, 1, 2)):
                for part in parts:
                    sp.dma_start(
                        raw[:, part, 0:size * D].rearrange("p (b n) -> p b n", b=size),
                        src[part][bass.ds(b0, size), :, :].rearrange("b p n -> p b n")
                    ).then_inc(raw_in, 16)

            sources = {"A": (t["w1a"], t["w3a"], w2_scratch), "B": (t["gate"], t["up"], t["down"]),
                       "S": (t["b"], None, t["c"])}
            sp.wait_ge(scratch_done, 64)
            first = True
            for li, kind in enumerate(LAYERS):
                if kind == "B" and LAYERS[li + 1:]:
                    sp.wait_ge(acc_free, tile_no[1, CH - 1] + TT)
                    sp.dma_start(skip_d[:, :], t["skip_d"]).then_inc(skip_in, 16)
                b0 = 0
                for g, size in enumerate(SIZES[kind]):
                    if kind == "A" and g:
                        break
                    if not first:
                        before = previous(li, g) or (0, len(SIZES["A"]) - 1)
                        sp.wait_ge(w_ready, parts_no[before])
                    load(sources[kind], b0, size, (0, 2) if kind == "S" else (0, 1, 2))
                    b0 += size
                    if first:
                        first = False
                        sp.wait_ge(halt_x, 1)
                        for c in range(1, CH):
                            sp.dma_start(x[:, c * TT:(c + 1) * TT, :],
                                         t["x"][:, c * TT:(c + 1) * TT, :]).then_inc(x_in[c], 16)
                if kind == "A":
                    with sp.Fori(1, len(SIZES["A"])) as g:
                        sp.wait_ge(w_ready, (parts_no[li, 0] - 3) + g * 3)
                        load(sources[kind], g * 2, 2)
            for c in range(CH):
                sp.wait_ge(acc_free, tile_no[LAST, len(SIZES["B"]) - 1, c] + TT)
                sp.dma_start(t["out"][:, c * TT:(c + 1) * TT, :],
                             x[:, c * TT:(c + 1) * TT, :]).then_inc(out_done, 16)
            sp.wait_ge(out_done, 16 * CH)

        @block.tensor
        def _(pe):
            pe.wait_ge(had_ready, 2)
            for s in range(4):
                pe.wait_ge(fw_ready, s + 1)
                at = 1 + s % 3
                banks = acc if s % 2 else work
                for j in range(4):
                    if s >= 2:
                        pe.wait_ge(fw_out, 4 * (s - 2) + j + 1)
                    for i in range(4):
                        sign = neg_had if bin(i & j).count("1") % 2 else had
                        pe.matmul(banks[:, j, :], sign, xT_hi[:, at, i, :], start=i == 0, stop=False)
                        last = pe.matmul(banks[:, j, :], sign, xT_lo[:, at, i, :],
                                         start=False, stop=i == 3)
                    last.then_inc(fw_full, 1)
            for m in range(2):
                pe.wait_ge(att_w_ready, 2 * m + 2)
                a, b = att_at[2 * m], att_at[2 * m + 1]
                banks = acc if m else work
                pe.wait_ge(fw_out, 12 + 4 * m)
                for k in range(KD):
                    for j in range(KD):
                        last = three(pe, banks[:, k, :],
                                     xT_hi[:, a, j, k * P:(k + 1) * P], xT_lo[:, a, j, k * P:(k + 1) * P],
                                     xT_hi[:, b, j, :], xT_lo[:, b, j, :], j == 0, j == KD - 1)
                    last.then_inc(mix_full, 1)
            pe.wait_ge(mix_ready, 2 * KD)

            xn_pairs = [0]

            def pair_wait(w):
                if isinstance(w, int) and w < 2:
                    return
                pe.wait_ge(pair_free, w - 1)

            def transpose_pair(key):
                w = use[key]
                pair_wait(w)
                xn_pairs[0] += 1
                pe.wait_ge(xn_ready, 2 * xn_pairs[0])
                for j in range(2):
                    for k in range(KD):
                        last = pe.transpose(work[:, w % 2 * 2 + j, k * P:(k + 1) * P],
                                            xn[j][:, k * P:(k + 1) * P], ident[:, :])
                last.then_inc(pair_full, 1)

            def up(w, pair, c, buf, b, matrices):
                pair_wait(w)
                for m in range(matrices):
                    for k in range(KD):
                        at = slice(b * D + k * P, b * D + (k + 1) * P)
                        last = three(pe, work[:, 2 * pair + m, :], w_hi[buf][:, m, at], w_lo[buf][:, m, at],
                                     xT_hi[:, c, k, :], xT_lo[:, c, k, :], k == 0, k == KD - 1)
                last.then_inc(pair_full, 1)

            def down(n, h, buf, b, size, tile):
                pe.wait_ge(hid_lo_ready, n + 1)
                at = slice(b * D, (b + 1) * D)
                for i in range(TT):
                    if b == 0 and not (isinstance(tile, int) and tile < TT):
                        pe.wait_ge(acc_free, tile - 3 + i)
                    ts = slice(i * P, (i + 1) * P)
                    last = three(pe, acc[:, i, :], hid_hi[h][:, ts], hid_lo[h][:, ts],
                                 w_hi[buf][:, 2, at], w_lo[buf][:, 2, at], b == 0, b == size - 1)
                    if b == size - 1:
                        last.then_inc(acc_ready, 1)

            def step(li, g, c0, c, d=0, dt=0):
                kind = LAYERS[li]
                size, buf = SIZES[kind][g], group_buffer(li, g)
                for b in range(size):
                    w, n = use[li, g, c0, b], block_no[li, g, c0, b]
                    up(w + d, w % 2, c, buf, b, 1 if kind == "S" else 2)
                    if b:
                        down(n - 1 + d, (n - 1) % 2, buf, b - 1, size, tile_no[li, g, c0] + dt)
                    elif c0:
                        down(n - 1 + d, (n - 1) % 2, buf, size - 1, size, tile_no[li, g, c0] - TT + dt)
                    elif previous(li, g):
                        lp, gp = previous(li, g)
                        sp_ = SIZES[LAYERS[lp]][gp]
                        down(n - 1 + d, (n - 1) % 2, group_buffer(lp, gp), sp_ - 1, sp_,
                             tile_no[li, g, c0] - TT + dt)
                    if (li, g, c0, b) in plan.after:
                        transpose_pair(plan.after[li, g, c0, b])

            def group(li, g, d=0, dt=0, dp=0):
                pe.wait_ge(w_ready, parts_no[li, g] + dp)
                if g == 0:
                    pe.wait_ge(pair_free, use["x", li, 0, 1] + 1)
                step(li, g, 0, 0, d, dt)
                G = len(SIZES[LAYERS[li]])
                if g in (0, G - 1) or SIZES[LAYERS[li]][g] == 1:
                    for c in range(1, CH):
                        if g == 0:
                            pe.wait_ge(pair_free, use["x", li, c, 1] + 1)
                        step(li, g, c, c, d, dt)
                else:
                    with pe.Fori(0, CH - 1) as e:
                        step(li, g, 1, e + 1, e * 2 + d, e * TT + dt)

            def q_pair(c, j):
                w = use["q", c, j]
                pair_wait(w)
                for i in range(2):
                    m = slice((2 * j + i) * P, (2 * j + i + 1) * P)
                    for k in range(KD):
                        last = three(pe, work[:, w % 2 * 2 + i, :], mix_hi[:, 0, k, m], mix_lo[:, 0, k, m],
                                     xT_hi[:, c, k, :], xT_lo[:, c, k, :], k == 0, k == KD - 1)
                last.then_inc(pair_full, 1)

            def v_pair(c, j):
                w = use["v", c, j]
                pair_wait(w)
                for i in range(2):
                    m = slice((2 * j + i) * P, (2 * j + i + 1) * P)
                    for k in range(KD):
                        last = three(pe, work[:, w % 2 * 2 + i, :], xT_hi[:, c, k, m], xT_lo[:, c, k, m],
                                     mix_hi[:, 1, k, :], mix_lo[:, 1, k, :], k == 0, k == KD - 1)
                last.then_inc(pair_full, 1)

            def scores(c, i):
                pe.wait_ge(acc_free, tile_no[1, c] - 3 + i)
                n = (i + 1) * P
                for k in range(KD):
                    last = three(pe, acc[:, i, 0:n], qT_hi[:, k, i * P:n], qT_lo[:, k, i * P:n],
                                 xT_hi[:, c, k, 0:n], xT_lo[:, c, k, 0:n], k == 0, k == KD - 1)
                last.then_inc(score_ready, 1)

            def p_transpose(c, i):
                w = use["p", c, i]
                pair_wait(w)
                pe.wait_ge(exp_ready, TT * c + i + 1)
                for k in range(i + 1):
                    last = pe.transpose(work[:, w % 2 * 2, k * P:(k + 1) * P],
                                        hid[i % 2][:, k * P:(k + 1) * P], ident[:, :])
                last.then_inc(pair_full, 1)

            def attend(c, i):
                pe.wait_ge(pair_free, use["p", c, i] + 1)
                for k in range(i + 1):
                    ks = slice(k * P, (k + 1) * P)
                    last = three(pe, acc[:, i, :], hid_hi[i % 2][:, ks], hid_lo[i % 2][:, ks],
                                 v_hi[:, k, :], v_lo[:, k, :], k == 0, k == i)
                last.then_inc(acc_ready, 1)

            def attention(li):
                pe.wait_ge(pair_free, use["x", li, 0, 1] + 1)
                q_pair(0, 0)
                lp, gp = li - 1, len(SIZES[LAYERS[li - 1]]) - 1
                n = block_no[lp, gp, CH - 1, 1]
                down(n, n % 2, group_buffer(lp, gp), 1, 2, tile_no[lp, gp, CH - 1])
                q_pair(0, 1)
                for c in range(CH):
                    more = c + 1 < CH
                    first = ("x", 1, c + 2) if c < 2 else ("x", 2, c - 1)
                    pe.wait_ge(pair_free, use["q", c, 1] + 1)
                    for i in range(TT):
                        scores(c, i)
                    v_pair(c, 0)
                    p_transpose(c, 0)
                    v_pair(c, 1)
                    transpose_pair(first + (0,))
                    p_transpose(c, 1)
                    if more:
                        pe.wait_ge(pair_free, use["x", li, c + 1, 1] + 1)
                        q_pair(c + 1, 0)
                    attend(c, 0)
                    p_transpose(c, 2)
                    transpose_pair(first + (1,))
                    if more:
                        q_pair(c + 1, 1)
                    attend(c, 1)
                    p_transpose(c, 3)
                    if c == 1:
                        transpose_pair(("x", 2, 0, 0))
                    attend(c, 2)
                    if c == 1:
                        transpose_pair(("x", 2, 0, 1))
                    attend(c, 3)

            pe.wait_ge(consts_in, 80)
            for c in (0, 1):
                for half in (0, 1):
                    transpose_pair(("x", 0, c, half))
            for li, kind in enumerate(LAYERS):
                G = len(SIZES[kind])
                if kind == "T":
                    attention(li)
                elif kind == "A":
                    group(li, 0)
                    with pe.Fori(0, (G - 2) // 2) as o:
                        group(li, 1, o * 16, o * 32, o * 6)
                        group(li, 2, o * 16, o * 32, o * 6)
                    group(li, G - 1)
                else:
                    for g in range(G):
                        group(li, g)
            g = len(SIZES["B"]) - 1
            n = block_no[LAST, g, CH - 1, 1]
            down(n, n % 2, group_buffer(LAST, g), 1, 2, tile_no[LAST, g, CH - 1])

        @block.scalar
        def _(act):
            act.wait_ge(consts_in, 80)
            nc.scalar.activation(had, hid[0][:, 0:P], ACT.Copy).then_inc(had_ready, 1)
            nc.scalar.activation(neg_had, hid[0][:, 0:P], ACT.Copy, scale=-1.0).then_inc(had_ready, 1)

            def fw_split(s):
                act.wait_ge(fly_ready, s + 1)
                if s == 3:
                    act.wait_ge(fw_full, 4)
                nc.scalar.activation(xT_hi[:, 1 + s % 3, :, :], fw_buf[s % 2],
                                     ACT.Copy).then_inc(fw_hi_ready, 1)

            def fw_scale(s):
                for j in range(4):
                    act.wait_ge(fw_full, 4 * s + j + 1)
                    if s and j == 0:
                        act.wait_ge(scratch_done, 16 * s)
                    bank = (acc if s % 2 else work)[:, j, :]
                    nc.scalar.activation(raw[:, j // 2, j % 2 * D:(j % 2 + 1) * D], bank, ACT.Copy,
                                         scale=0.5 * HA ** -0.5).then_inc(fw_out, 1)

            for s in range(4):
                fw_split(s)
                if s:
                    fw_scale(s - 1)
            fw_scale(3)
            for i in range(4):
                act.wait_ge(att_w_in[i], 16)
                act.wait_ge(fw_full, 16)
                if i == 3:
                    act.wait_ge(mix_full, KD)
                nc.scalar.activation(xT_hi[:, att_at[i], :, :], att_raw[i], ACT.Copy).then_inc(att_w_hi, 1)
            for m in range(2):
                for k in range(KD):
                    act.wait_ge(mix_full, KD * m + k + 1)
                    nc.scalar.activation(mix_hi[:, m, k, :], (acc if m else work)[:, k, :],
                                         ACT.Copy).then_inc(mix_hi_ready, 1)

            affine_pairs = [0]
            w_parts = [0]

            def split_part(li, g, part, prepared=0):
                size, buf = SIZES[LAYERS[li]][g], group_buffer(li, g)
                nc.scalar.activation(w_hi[buf][:, part, 0:size * D], raw[:, part, 0:size * D],
                                     ACT.Copy).then_inc(w_hi_ready, 1)

            def weights_here(li, g, dr=0):
                act.wait_ge(raw_in, raw_count[li, g] + dr)
                if LAYERS[li] == "B":
                    act.wait_ge(w_scaled, scaled_count[li, g])

            def up(w, pair, n, h, li, blk):
                act.wait_ge(pair_full, w + 1)
                if LAYERS[li] == "S":
                    nc.scalar.activation(hid[h][:, :], work[:, 2 * pair, :], ACT.Tanh).then_inc(act_ready, 1)
                    return
                scale = gate_s[:, blk:blk + 1] if LAYERS[li] == "B" else 1.0
                nc.scalar.activation(hid[h][:, :], work[:, 2 * pair, :], ACT.Silu,
                                     scale=scale).then_inc(act_ready, 1)
                act.wait_ge(pair_free, w + 1)
                nc.scalar.activation(hid_hi[h][:, :], hid[h][:, :], ACT.Copy).then_inc(hid_hi_ready, 1)

            def transpose_pair(key):
                w = use[key]
                act.wait_ge(pair_full, w + 1)
                if LAYERS[key[1]] == "T":
                    affine_pairs[0] += 1
                    act.wait_ge(affine_ready, affine_pairs[0])
                for j in range(2):
                    ts = slice((2 * key[3] + j) * P, (2 * key[3] + j + 1) * P)
                    nc.scalar.activation(
                        xT_hi[:, key[2], :, ts],
                        work[:, w % 2 * 2 + j, :].rearrange("p (k t) -> p k t", k=KD),
                        ACT.Copy).then_inc(xT_hi_ready, 1)

            def step(li, g, c0, c, d=0, dr=0):
                for b in range(SIZES[LAYERS[li]][g]):
                    w, n = use[li, g, c0, b], block_no[li, g, c0, b]
                    up(w + d, w % 2, n + d, n % 2, li, sum(SIZES[LAYERS[li]][:g]) + b)
                    if c0 and b == 0 and following(li, g):
                        ln, gn = following(li, g)
                        if not isinstance(c, int):
                            if c0 == 1:
                                weights_here(ln, gn, dr)
                            split_part(ln, gn, c - 1)
                        elif not (LAYERS[ln] == "S" and c == 2):
                            weights_here(ln, gn, dr)
                            split_part(ln, gn, c - 1)
                    if (li, g, c0, b) in plan.after:
                        transpose_pair(plan.after[li, g, c0, b])

            def group(li, g, d=0, dr=0):
                step(li, g, 0, 0, d, dr)
                G = len(SIZES[LAYERS[li]])
                if g in (0, G - 1) or SIZES[LAYERS[li]][g] == 1:
                    for c in range(1, CH):
                        step(li, g, c, c, d, dr)
                else:
                    with act.Fori(0, CH - 1) as e:
                        step(li, g, 1, e + 1, e * 2 + d, dr)

            def pair_hi(key, dst):
                w = use[key]
                act.wait_ge(pair_full, w + 1)
                for i in range(2):
                    nc.scalar.activation(dst[:, 2 * key[2] + i, :], work[:, w % 2 * 2 + i, :],
                                         ACT.Copy).then_inc(att_hi_ready, 1)

            def numerators(c, i):
                act.wait_ge(max_ready, TT * c + i + 1)
                if i >= 2:
                    act.wait_ge(pair_full, use["p", c, i - 2] + 1)
                n = (i + 1) * P
                nc.scalar.activation(hid[i % 2][:, 0:n], acc[:, i, 0:n], ACT.Exp,
                                     bias=negmax[:, i:i + 1], scale=SCORE_SCALE,
                                     accum_out=rowsum[:, i:i + 1]).then_inc(exp_ready, 1)

            def p_hi(c, i):
                w = use["p", c, i]
                act.wait_ge(pair_full, w + 1)
                if i >= 2:
                    act.wait_ge(acc_ready, tile_no[1, c] + i - 1)
                n = (i + 1) * P
                nc.scalar.activation(hid_hi[i % 2][:, 0:n], work[:, w % 2 * 2, 0:n],
                                     ACT.Copy).then_inc(att_hi_ready, 1)

            def attention(li):
                for j in range(2):
                    pair_hi(("q", 0, j), qT_hi)
                for c in range(CH):
                    more = c + 1 < CH
                    first = ("x", 1, c + 2) if c < 2 else ("x", 2, c - 1)
                    numerators(c, 0)
                    numerators(c, 1)
                    pair_hi(("v", c, 0), v_hi)
                    p_hi(c, 0)
                    pair_hi(("v", c, 1), v_hi)
                    transpose_pair(first + (0,))
                    p_hi(c, 1)
                    numerators(c, 2)
                    if more:
                        pair_hi(("q", c + 1, 0), qT_hi)
                    numerators(c, 3)
                    p_hi(c, 2)
                    transpose_pair(first + (1,))
                    if more:
                        pair_hi(("q", c + 1, 1), qT_hi)
                    else:
                        weights_here(li + 1, 0)
                        for part in range(3):
                            split_part(li + 1, 0, part)
                    p_hi(c, 3)
                    if c == 1:
                        transpose_pair(("x", 2, 0, 0))
                        transpose_pair(("x", 2, 0, 1))

            weights_here(0, 0)
            for part in range(3):
                split_part(0, 0, part)
            for c in (0, 1):
                for half in (0, 1):
                    transpose_pair(("x", 0, c, half))
            for li, kind in enumerate(LAYERS):
                G = len(SIZES[kind])
                if kind == "T":
                    attention(li)
                elif kind == "A":
                    group(li, 0)
                    with act.Fori(0, (G - 2) // 2) as o:
                        group(li, 1, o * 16, o * 96)
                        group(li, 2, o * 16, o * 96)
                    group(li, G - 1)
                else:
                    for g in range(G):
                        group(li, g)

        @block.gpsimd
        def _(pool):
            pool.memset(minus_half[:, :], -0.5).then_inc(pool_step, 1)
            steps = [1]

            def deviation(out, var, n):
                pool.tensor_scalar(var_eps[:, 0:n], var, 1.0, EPS, ALU.mult, ALU.add).then_inc(pool_step, 1)
                steps[0] += 1
                pool.wait_ge(pool_step, steps[0])
                return pool.tensor_tensor(out, var_eps[:, 0:n], minus_half[:, 0:n], ALU.pow)

            done, done2 = [0], [0]

            def var_eps_read():
                if done[0]:
                    pool.wait_ge(rstd_ready, done[0])
                if done2[0]:
                    pool.wait_ge(rstd2_ready, done2[0])

            def chunk(c):
                var_eps_read()
                done[0] += 1
                pool.wait_ge(stats_ready, done[0])
                deviation(rstd[:, c * TT:(c + 1) * TT], meanvar[:, c * TT:(c + 1) * TT, 1], TT
                          ).then_inc(rstd_ready, 1)

            def second():
                var_eps_read()
                done2[0] += 1
                pool.wait_ge(stats2_ready, done2[0])
                deviation(rstd2[:, :], meanvar2[:, :, 1], 2).then_inc(rstd2_ready, 1)

            for c in range(CH):
                chunk(c)
            for li in range(1, LAST + 1):
                if LAYERS[li] != "T":
                    for c in range(CH if LAYERS[li - 1] != "T" else 1):
                        chunk(c)
                    if LAYERS[li - 1] == "T":
                        second()
                        second()
                        for c in range(1, CH):
                            chunk(c)
                else:
                    chunk(0)
                    second()
                    for c in range(1, CH):
                        chunk(c)
                        second()
                        if c < CH - 1:
                            second()

        @block.vector
        def _(dve):
            steps = [0]

            def link(ins):
                steps[0] += 1
                ins.then_inc(dve_step, 1)
                dve.wait_ge(dve_step, steps[0])

            chunks = [0]

            def norm_stats(li, c, first=False):
                if chunks[0]:
                    dve.wait_ge(stats_ready, chunks[0])
                chunks[0] += 1
                if first:
                    dve.wait_ge(x_in[c], 16)
                for i in range(TT):
                    last = nc.vector.bn_stats(stats[:, i, :], x[:, c * TT + i, :])
                link(last)
                for i in range(TT):
                    last = nc.vector.bn_aggr(meanvar[:, c * TT + i, :], stats[:, i, :])
                last.then_inc(stats_ready, 1)

            norm_stats(0, 0, True)

            def fly(dst, src, pattern):
                s = src.rearrange("p a (b d) -> p a b d", b=4)
                o = dst.rearrange("p a (b d) -> p a b d", b=4)
                if pattern == 0:
                    lo_s, hi_s, lo_o, hi_o = s[:, :, 0:4:2, :], s[:, :, 1:4:2, :], o[:, :, 0:4:2, :], o[:, :, 1:4:2, :]
                else:
                    lo_s, hi_s, lo_o, hi_o = s[:, :, 0:2, :], s[:, :, 2:4, :], o[:, :, 0:2, :], o[:, :, 2:4, :]
                nc.vector.tensor_tensor(lo_o, lo_s, hi_s, ALU.add)
                return nc.vector.tensor_tensor(hi_o, lo_s, hi_s, ALU.subtract)

            def fw_lo(s):
                dve.wait_ge(fw_hi_ready, s + 1)
                nc.vector.tensor_tensor(xT_lo[:, 1 + s % 3, :, :], fw_buf[s % 2],
                                        xT_hi[:, 1 + s % 3, :, :], ALU.subtract).then_inc(fw_ready, 1)

            for s in range(4):
                dve.wait_ge(fw_in[s], 16)
                link(fly(fw_tmp, fw_buf[s % 2], 0))
                fly(fw_buf[s % 2], fw_tmp, 1).then_inc(fly_ready, 1)
                fw_lo(s)
                dve.wait_ge(fw_ready, s + 1)
                dve.engine_nop().then_inc(fw_taken, 1)
            for i in range(4):
                dve.wait_ge(att_w_hi, i + 1)
                nc.vector.tensor_tensor(xT_lo[:, att_at[i], :, :], att_raw[i],
                                        xT_hi[:, att_at[i], :, :], ALU.subtract).then_inc(att_w_ready, 1)
            dve.wait_ge(att_w_ready, 4)
            dve.engine_nop().then_inc(halt_x, 1)
            for m in range(2):
                for k in range(KD):
                    dve.wait_ge(mix_hi_ready, KD * m + k + 1)
                    nc.vector.tensor_tensor(mix_lo[:, m, k, :], (acc if m else work)[:, k, :],
                                            mix_hi[:, m, k, :], ALU.subtract).then_inc(mix_ready, 1)
            dve.wait_ge(consts_in, 80)
            link(nc.vector.tensor_scalar(half_down_s[:, :], half_down_s[:, :], 0.5, None, ALU.mult))

            normed, normed2, hi_tiles, att_his, w_part, rstds = [0], [0], [0], [0], [0], {}

            def normalise(key):
                _, li, c, half = key
                dve.wait_ge(rstd_ready, 4 * li + c + 1)
                kind = LAYERS[li]
                for j in range(2):
                    i = c * TT + 2 * half + j
                    last = nc.vector.tensor_scalar(xn[j][:, :], x[:, i, :], meanvar[:, i, 0:1], rstd[:, i:i + 1],
                                                   ALU.subtract, ALU.mult)
                    if kind != "T" and kind != "S":
                        last.then_inc(xn_ready, 1)
                if kind == "T":
                    link(last)
                    if normed2[0]:
                        dve.wait_ge(stats2_ready, normed2[0])
                    for j in range(2):
                        last = nc.vector.bn_stats(stats2[:, j, :], xn[j][:, :])
                    link(last)
                    for j in range(2):
                        last = nc.vector.bn_aggr(meanvar2[:, j, :], stats2[:, j, :])
                    last.then_inc(stats2_ready, 1)
                    for j in range(2):
                        i = c * TT + 2 * half + j
                        last = nc.vector.tensor_tensor(x[:, i, :], x[:, i, :], xn[j][:, :], ALU.add)
                    link(last)
                    normed2[0] += 1
                    dve.wait_ge(rstd2_ready, normed2[0])
                    for j in range(2):
                        nc.vector.tensor_scalar(xn[j][:, :], xn[j][:, :], meanvar2[:, j, 0:1], rstd2[:, j:j + 1],
                                                ALU.subtract, ALU.mult).then_inc(xn_ready, 1)
                if kind == "S":
                    link(last)
                    dve.wait_ge(skip_in, 16)
                    for j in range(2):
                        i = c * TT + 2 * half + j
                        link(nc.vector.tensor_tensor(skip_t, xn[j][:, :], skip_d[:, :], ALU.mult))
                        nc.vector.tensor_tensor(x[:, i, :], x[:, i, :], skip_t, ALU.add).then_inc(xn_ready, 1)
                        dve.wait_ge(xn_ready, 2 * normed[0] + j + 1)
                normed[0] += 1

            def transpose_pair(key):
                w = use[key]
                if LAYERS[key[1]] == "T":
                    dve.wait_ge(pair_full, w + 1)
                    for k in range(KD):
                        bank = work[:, w % 2 * 2:w % 2 * 2 + 2, k * P:(k + 1) * P]
                        last = nc.vector.tensor_scalar(bank, bank, gamma[:, k:k + 1], beta[:, k:k + 1],
                                                       ALU.mult, ALU.add)
                    last.then_inc(affine_ready, 1)
                for j in range(2):
                    hi_tiles[0] += 1
                    dve.wait_ge(xT_hi_ready, hi_tiles[0])
                    ts = slice((2 * key[3] + j) * P, (2 * key[3] + j + 1) * P)
                    last = nc.vector.tensor_tensor(
                        xT_lo[:, key[2], :, ts],
                        work[:, w % 2 * 2 + j, :].rearrange("p (k t) -> p k t", k=KD),
                        xT_hi[:, key[2], :, ts], ALU.subtract)
                last.then_inc(pair_free, 1)

            def up(w, pair, n, n_ffn, h, li, blk):
                dve.wait_ge(act_ready, n + 1)
                if LAYERS[li] == "S":
                    nc.vector.tensor_copy(hid_hi[h][:, :], hid[h][:, :]).then_inc(pair_free, 1)
                    dve.wait_ge(pair_free, w + 1)
                else:
                    scale = up_s[:, blk:blk + 1] if LAYERS[li] == "B" else 1.0
                    nc.vector.scalar_tensor_tensor(hid[h][:, :], work[:, 2 * pair + 1, :], scale, hid[h][:, :],
                                                   ALU.mult, ALU.mult).then_inc(pair_free, 1)
                    dve.wait_ge(hid_hi_ready, n_ffn + 1)
                nc.vector.tensor_tensor(hid_lo[h][:, :], hid[h][:, :], hid_hi[h][:, :],
                                        ALU.subtract).then_inc(hid_lo_ready, 1)

            def add_tiles(tile, c):
                for i in range(TT):
                    dve.wait_ge(acc_ready, tile + i + 1)
                    nc.vector.tensor_tensor(x[:, c * TT + i, :], acc[:, i, :], x[:, c * TT + i, :],
                                            ALU.add).then_inc(acc_free, 1)

            def split_part(li, g, part, no):
                size, buf = SIZES[LAYERS[li]][g], group_buffer(li, g)
                dve.wait_ge(w_hi_ready, no)
                nc.vector.tensor_tensor(w_lo[buf][:, part, 0:size * D], raw[:, part, 0:size * D],
                                        w_hi[buf][:, part, 0:size * D], ALU.subtract).then_inc(w_ready, 1)

            def scale_down(li, g):
                dve.wait_ge(raw_in, raw_count[li, g])
                for b in range(SIZES[LAYERS[li]][g]):
                    last = nc.vector.tensor_tensor(raw[:, 2, b * D:(b + 1) * D], raw[:, 2, b * D:(b + 1) * D],
                                                   half_down_s[:, :], ALU.mult)
                last.then_inc(w_scaled, 1)

            def finish_chunk(li, g, c):
                if li < LAST and g == len(SIZES[LAYERS[li]]) - 1:
                    dve.wait_ge(acc_free, tile_no[li, g, c] + TT)
                    norm_stats(li + 1, c)

            def step(li, g, c0, c, d=0, dt=0, dp=0, inner=0):
                kind = LAYERS[li]
                for b in range(SIZES[kind][g]):
                    w, n = use[li, g, c0, b], block_no[li, g, c0, b]
                    ffn_before = sum(SIZES["S"]) * CH if li > LAYERS.index("S") else 0
                    up(w + d, w % 2, n + d, n - ffn_before + d, n % 2, li, sum(SIZES[kind][:g]) + b)
                    if b == 0 and c0:
                        add_tiles(tile_no[li, g, c0] - TT + dt, c - 1)
                        if isinstance(c, int):
                            finish_chunk(li, g, c - 1)
                    elif b == 0 and previous(li, g):
                        add_tiles(tile_no[li, g, c0] - TT + dt, CH - 1)
                        if isinstance(c, int) and g == 0:
                            finish_chunk(*previous(li, g), CH - 1)
                    if b == 0 and following(li, g):
                        ln, gn = following(li, g)
                        base = parts_no[ln, gn] - (2 if LAYERS[ln] == "S" else 3)
                        if c0 == 0:
                            if LAYERS[ln] == "B":
                                scale_down(ln, gn)
                        elif LAYERS[ln] != "S":
                            split_part(ln, gn, c - 1, base + c + dp)
                        elif c != 2:
                            split_part(ln, gn, c - 1, base + (c + 1) // 2)
                    if (li, g, c0, b) in plan.after:
                        key = plan.after[li, g, c0, b]
                        transpose_pair(key)
                        if key[3] == 0:
                            normalise(key[:3] + (1,))
                if isinstance(c, int) and c and g == len(SIZES[kind]) - 1 and li < LAST:
                    normalise(("x", li + 1, c - 1, 0))
                if g == 0 and c0 == 0:
                    normalise(("x", li, CH - 1, 0))

            def group(li, g, d=0, dt=0, dp=0):
                step(li, g, 0, 0, d, dt, dp)
                G = len(SIZES[LAYERS[li]])
                if g in (0, G - 1) or SIZES[LAYERS[li]][g] == 1:
                    for c in range(1, CH):
                        step(li, g, c, c, d, dt, dp)
                else:
                    with dve.Fori(0, CH - 1) as e:
                        step(li, g, 1, e + 1, e * 2 + d, e * TT + dt, dp)

            def pair_lo(key, dst_hi, dst_lo):
                w = use[key]
                for i in range(2):
                    att_his[0] += 1
                    dve.wait_ge(att_hi_ready, att_his[0])
                    last = nc.vector.tensor_tensor(dst_lo[:, 2 * key[2] + i, :], work[:, w % 2 * 2 + i, :],
                                                   dst_hi[:, 2 * key[2] + i, :], ALU.subtract)
                last.then_inc(pair_free, 1)

            def maxima(c, i):
                dve.wait_ge(score_ready, TT * c + i + 1)
                n = (i + 1) * P
                link(nc.vector.tensor_tensor(acc[:, i, n - P:n], acc[:, i, n - P:n], causal[:, :], ALU.add))
                link(nc.vector.reduce_max(rowmax[:, i:i + 1], acc[:, i, 0:n], AX.X))
                nc.vector.tensor_scalar(negmax[:, i:i + 1], rowmax[:, i:i + 1], -SCORE_SCALE, None,
                                        ALU.mult).then_inc(max_ready, 1)

            def p_lo(c, i):
                w = use["p", c, i]
                att_his[0] += 1
                dve.wait_ge(att_hi_ready, att_his[0])
                n = (i + 1) * P
                nc.vector.tensor_tensor(hid_lo[i % 2][:, 0:n], work[:, w % 2 * 2, 0:n],
                                        hid_hi[i % 2][:, 0:n], ALU.subtract).then_inc(pair_free, 1)

            def attended(c, i):
                link(nc.vector.reciprocal(rowinv[:, i:i + 1], rowsum[:, i:i + 1]))
                dve.wait_ge(acc_ready, tile_no[1, c] + i + 1)
                nc.vector.scalar_tensor_tensor(x[:, c * TT + i, :], acc[:, i, :], rowinv[:, i:i + 1],
                                               x[:, c * TT + i, :], ALU.mult, ALU.add).then_inc(acc_free, 1)

            def attention(li):
                pair_lo(("q", 0, 0), qT_hi, qT_lo)
                lp, gp = li - 1, len(SIZES[LAYERS[li - 1]]) - 1
                add_tiles(tile_no[lp, gp, CH - 1], CH - 1)
                pair_lo(("q", 0, 1), qT_hi, qT_lo)
                finish_chunk(lp, gp, CH - 1)
                for c in range(CH):
                    more = c + 1 < CH
                    first = ("x", 1, c + 2) if c < 2 else ("x", 2, c - 1)
                    for i in range(TT):
                        maxima(c, i)
                    pair_lo(("v", c, 0), v_hi, v_lo)
                    p_lo(c, 0)
                    pair_lo(("v", c, 1), v_hi, v_lo)
                    transpose_pair(first + (0,))
                    normalise(first + (1,))
                    p_lo(c, 1)
                    if more:
                        pair_lo(("q", c + 1, 0), qT_hi, qT_lo)
                    attended(c, 0)
                    p_lo(c, 2)
                    transpose_pair(first + (1,))
                    if c == 1:
                        normalise(("x", 2, 0, 0))
                    if more:
                        pair_lo(("q", c + 1, 1), qT_hi, qT_lo)
                    else:
                        for part in range(3):
                            split_part(li + 1, 0, part, parts_no[li + 1, 0] - 2 + part)
                    attended(c, 1)
                    p_lo(c, 3)
                    if c == 1:
                        transpose_pair(("x", 2, 0, 0))
                        normalise(("x", 2, 0, 1))
                    attended(c, 2)
                    if c == 1:
                        transpose_pair(("x", 2, 0, 1))
                    attended(c, 3)
                    dve.wait_ge(acc_free, tile_no[li, c] + TT)
                    norm_stats(li + 1, c)
                    if c == 0:
                        normalise(("x", 1, CH - 1, 0))
                    elif c < CH - 1:
                        normalise(("x", 2, c, 0))

            for part in range(3):
                split_part(0, 0, part, part + 1)
            for c in (0, 1):
                if c:
                    for cc in range(1, CH):
                        norm_stats(0, cc, True)
                normalise(("x", 0, c, 0))
                transpose_pair(("x", 0, c, 0))
                normalise(("x", 0, c, 1))
                transpose_pair(("x", 0, c, 1))
            normalise(("x", 0, 2, 0))
            for li, kind in enumerate(LAYERS):
                G = len(SIZES[kind])
                if kind == "T":
                    attention(li)
                elif kind == "A":
                    group(li, 0)
                    with dve.Fori(0, (G - 2) // 2) as o:
                        group(li, 1, o * 16, o * 32, o * 6)
                        group(li, 2, o * 16, o * 32, o * 6)
                    group(li, G - 1)
                else:
                    for g in range(G):
                        group(li, g)
            add_tiles(tile_no[LAST, len(SIZES["B"]) - 1, CH - 1], CH - 1)


def _counts():
    raw, scaled, r, s = {}, {}, 0, 0
    for li, kind in enumerate(LAYERS):
        for g in range(len(SIZES[kind])):
            r += 32 if kind == "S" else 48
            s += kind == "B"
            raw[li, g], scaled[li, g] = r, s
    return raw, scaled


raw_count, scaled_count = _counts()


def kernel(**inputs):
    import concourse.bacc as bacc
    from concourse.bass_utils import run_bass_kernel_spmd

    a = {k: np.asarray(v) for k, v in inputs.items()}

    def up_blocks(w):
        h = w.shape[0]
        return w.reshape(h // P, P, KD, P).transpose(0, 3, 2, 1).reshape(h // P, P, KD * P)

    def down_blocks(w):
        return w.T.reshape(w.shape[1] // P, P, D)

    def rows(w):
        return w.reshape(KD, P, w.shape[1]).transpose(1, 0, 2)

    def column(v):
        return v.reshape(-1, P).T

    hadamard = np.array([[1.0]], np.float32)
    while len(hadamard) < P:
        hadamard = np.block([[hadamard, hadamard], [hadamard, -hadamard]])
    causal = np.where(np.arange(P)[None, :] <= np.arange(P)[:, None], 0.0, MASKED).astype(np.float32)
    qkv = a["L0_attn_qkv"]
    arrays = {
        "x": a["L0_attn_x"].reshape(CH * TT, P, D).transpose(1, 0, 2),
        "w1a": up_blocks(a["L0_ffn_W1"]),
        "w3a": up_blocks(a["L0_ffn_W3"]),
        "w2a": a["L0_ffn_W2"].reshape(4, P, HA // P, P).transpose(0, 3, 2, 1),
        "att_w": np.stack([rows(qkv[:, 0:D].T), rows(qkv[:, D:2 * D].T), rows(qkv[:, 2 * D:].T),
                           rows(a["L0_attn_o_proj"])]),
        "gate": up_blocks(a["L1_ffn_gate_w"]),
        "up": up_blocks(a["L1_ffn_up_w"]),
        "down": down_blocks(a["L1_ffn_down_w"]),
        "b": up_blocks(a["L1_attn_B"]),
        "c": down_blocks(a["L1_attn_C"]),
        "small": np.concatenate([column(a["L0_attn_gamma"]), column(a["L0_attn_beta"]),
                                 column(a["L1_ffn_gate_s"]), column(a["L1_ffn_up_s"])], axis=1),
        "down_s": np.broadcast_to(a["L1_ffn_down_s"][None, :], (P, D)),
        "skip_d": np.broadcast_to(a["L1_attn_D"][None, :], (P, D)),
        "ident": np.eye(P, dtype=np.float32),
        "hadamard": hadamard,
        "causal": causal,
    }
    arrays = {k: np.ascontiguousarray(v) for k, v in arrays.items()}
    nc = bacc.Bacc("TRN2", target_bir_lowering=False, num_devices=1)
    t = {k: nc.dram_tensor(f"in_{k}", v.shape, F32, kind="ExternalInput").ap() for k, v in arrays.items()}
    t["out"] = nc.dram_tensor("out_x", (P, CH * TT, D), F32, kind="ExternalOutput").ap()
    build(nc, t)
    r = run_bass_kernel_spmd(nc, [{f"in_{k}": v for k, v in arrays.items()}], core_ids=[0])
    out = r.results[0]["out_x"]
    return np.ascontiguousarray(out.transpose(1, 0, 2).reshape(CH, TOK, D))
```

```python
from contextlib import ExitStack

import numpy as np

import concourse.bass as bass
import concourse.mybir as mybir
from concourse.alu_op_type import AluOpType as ALU

F32 = mybir.dt.float32
F32R = mybir.dt.float32r
U32 = mybir.dt.uint32
I32 = mybir.dt.int32
MAX = bass.bass_isa.ReduceOp.max
LOW_BITS = 0xFFF
ACT = mybir.ActivationFunctionType
AX = mybir.AxisListType

P = 128
D = 512
KD = D // P
CH = 4
TOK = 512
TT = TOK // P
HA = 2048
HB = 1408
HS = 256
EPS = 1e-5
SCORE_SCALE = D ** -0.5
MASKED = -3e38

SIZES = {"A": [2] * (HA // 256), "B": [2, 2, 2, 2, 1, 2], "S": [2], "T": []}
LAYERS = ["A", "T", "A", "B", "S", "B"]
LAST = len(LAYERS) - 1
assert sum(SIZES["A"]) * P == HA and sum(SIZES["B"]) * P == HB and sum(SIZES["S"]) * P == HS


class Plan:

    def __init__(self):
        self.use, self.block, self.tile, self.parts = {}, {}, {}, {}
        self.after = {}
        use = block = tile = parts = 0
        for c in (0, 1):
            for half in (0, 1):
                self.use["x", 0, c, half] = use
                use += 1
        for li, kind in enumerate(LAYERS):
            if kind == "T":
                for j in (0, 1):
                    self.use["q", 0, j] = use
                    use += 1
                for c in range(CH):
                    self.tile[li, c] = tile
                    tile += TT
                    for key in attention_uses(c):
                        self.use[key] = use
                        use += 1
                continue
            sizes = SIZES[kind]
            for g, size in enumerate(sizes):
                parts += 2 if kind == "S" else 3
                self.parts[li, g] = parts
                for c in range(CH):
                    self.tile[li, g, c] = tile
                    tile += TT
                    for b in range(size):
                        self.use[li, g, c, b] = use
                        self.block[li, g, c, b] = block
                        use, block = use + 1, block + 1
                        key = None
                        if g == 0 and c in (0, 1) and not (c == 0 and li and LAYERS[li - 1] == "T"):
                            key = ("x", li, c + 2, b)
                        if g == len(sizes) - 1 and c in (2, 3) and li < LAST:
                            key = ("x", li + 1, c - 2, b)
                        if key:
                            self.after[li, g, c, b] = key
                            self.use[key] = use
                            use += 1
        self.tiles = tile


def attention_uses(c):
    first = ("x", 1, c + 2) if c < 2 else ("x", 2, c - 1)
    keys = [("v", c, 0), ("p", c, 0), ("v", c, 1), first + (0,), ("p", c, 1)]
    keys += [("q", c + 1, 0)] if c + 1 < CH else []
    keys += [("p", c, 2), first + (1,)]
    keys += [("q", c + 1, 1)] if c + 1 < CH else []
    keys += [("p", c, 3)]
    keys += [("x", 2, 0, 0), ("x", 2, 0, 1)] if c == 1 else []
    return keys


def previous(li, g):
    if g:
        return li, g - 1
    if li == 0 or LAYERS[li - 1] == "T":
        return None
    return li - 1, len(SIZES[LAYERS[li - 1]]) - 1


def following(li, g):
    if g + 1 < len(SIZES[LAYERS[li]]):
        return li, g + 1
    if li == LAST or LAYERS[li + 1] == "T":
        return None
    return li + 1, 0


def group_buffer(li, g):
    return (sum(len(SIZES[k]) for k in LAYERS[:li]) + g) % 2


def build(nc, t):
    plan = Plan()
    use, block_no, tile_no, parts_no = plan.use, plan.block, plan.tile, plan.parts

    w2_scratch = nc.dram_tensor("w2_scratch", [HA // P, P, D], F32).ap()

    with ExitStack() as ctx:
        def sb(name, shape, dt=F32):
            return ctx.enter_context(nc.sbuf_tensor(name, shape, dt))

        def sem(name):
            return ctx.enter_context(nc.semaphore(name))

        mix_at = -(-nc.sbuf_base // 64) * 64
        mix_hi = sb("mix_hi", [P, 2, KD, D], F32R)
        mix_lo = sb("mix_lo", [P, 2, KD, D], F32R)
        x = sb("x", [P, CH * TT, D])
        xT_hi = sb("xT_hi", [P, CH, KD, TOK], F32R)
        xT_lo = sb("xT_lo", [P, CH, KD, TOK], F32R)
        raw = sb("raw", [P, 3, 2 * D])
        w_hi = [sb(f"w_hi{i}", [P, 3, 2 * D], F32R) for i in range(2)]
        w_lo = [sb(f"w_lo{i}", [P, 3, 2 * D], F32R) for i in range(2)]
        hid = [sb(f"hid{i}", [P, TOK]) for i in range(2)]
        hid_hi = [sb(f"hid_hi{i}", [P, TOK], F32R) for i in range(2)]
        hid_lo = [sb(f"hid_lo{i}", [P, TOK], F32R) for i in range(2)]
        xn = [sb(f"xn{i}", [P, D]) for i in range(2)]
        ident = sb("ident", [P, P])
        causal = sb("causal", [P, P])
        half_down_s = sb("half_down_s", [P, D])
        skip_d = nc.alloc_sbuf_tensor_at("skip_d", [P, D], F32, offset=mix_at)
        low_bits = nc.alloc_sbuf_tensor_at("low_bits", [P, 3, 2 * D], U32, offset=mix_at + 8 * D)
        scaled = nc.alloc_sbuf_tensor_at("scaled", [P, TT, D], F32, offset=mix_at + 32 * D)
        skip_t = nc.alloc_sbuf_tensor_at("skip_t", [P, D], F32, offset=mix_at + 4 * D)[:, :]
        small = sb("small", [P, 2 * KD + 2 * (HB // P)])
        gamma, beta = small[:, 0:KD], small[:, KD:2 * KD]
        gate_s = small[:, 2 * KD:2 * KD + HB // P]
        up_s = small[:, 2 * KD + HB // P:]
        stats = sb("stats", [P, TT, 6])
        meanvar = sb("meanvar", [P, CH * TT, 2])
        rstd = sb("rstd", [P, CH * TT])
        stats2 = sb("stats2", [P, 2, 6])
        meanvar2 = sb("meanvar2", [P, 2, 2])
        rstd2 = sb("rstd2", [P, 2])
        var_eps = sb("var_eps", [P, TT])
        minus_half = sb("minus_half", [P, TT])
        low_max = sb("low_max", [P, len(SIZES["B"])])
        inexact = sb("inexact", [P, len(SIZES["B"])], I32)
        rowmax = sb("rowmax", [P, TT])
        negmax = sb("negmax", [P, TT])
        rowsum = sb("rowsum", [P, TT])
        rowinv = sb("rowinv", [P, TT])

        qT_hi = w_hi[0][:, 0:2, :].rearrange("p a (k t) -> p (a k) t", k=2)
        qT_lo = w_lo[0][:, 0:2, :].rearrange("p a (k t) -> p (a k) t", k=2)
        v_hi = w_hi[1][:, 0:2, :].rearrange("p a (k t) -> p (a k) t", k=2)
        v_lo = w_lo[1][:, 0:2, :].rearrange("p a (k t) -> p (a k) t", k=2)

        work = ctx.enter_context(nc.psum_tensor("work", [P, 4, D], F32))
        acc = ctx.enter_context(nc.psum_tensor("acc", [P, 4, D], F32))

        consts_in = sem("consts_in")
        x_in = [sem(f"x_in{c}") for c in range(CH)]
        raw_in = sem("raw_in")
        pair_full = sem("pair_full")
        pair_free = sem("pair_free")
        act_ready = sem("act_ready")
        hid_hi_ready = sem("hid_hi_ready")
        hid_lo_ready = sem("hid_lo_ready")
        acc_ready = sem("acc_ready")
        acc_free = sem("acc_free")
        w_hi_ready = sem("w_hi_ready")
        w_ready = sem("w_ready")
        low_ready = sem("low_ready")
        flag_ready = sem("flag_ready")
        x_added = sem("x_added")
        xn_ready = sem("xn_ready")
        xT_hi_ready = sem("xT_hi_ready")
        affine_ready = sem("affine_ready")
        stats_ready = sem("stats_ready")
        rstd_ready = sem("rstd_ready")
        stats2_ready = sem("stats2_ready")
        rstd2_ready = sem("rstd2_ready")
        att_hi_ready = sem("att_hi_ready")
        score_ready = sem("score_ready")
        max_ready = sem("max_ready")
        exp_ready = sem("exp_ready")
        dve_step = sem("dve_step")
        pool_step = sem("pool_step")
        skip_in = sem("skip_in")
        down_s_in = sem("down_s_in")
        out_done = sem("out_done")
        fw_in = [sem(f"fw_in{i}") for i in range(4)]
        had_in = sem("had_in")
        first_in = sem("first_in")
        had_ready = sem("had_ready")
        fw_hi_ready = sem("fw_hi_ready")
        fw_ready = sem("fw_ready")
        fw_full = sem("fw_full")
        fw_out = sem("fw_out")
        scratch_done = [sem(f"scratch_done{j}") for j in range(4)]
        fly_ready = sem("fly_ready")
        att_w_in = [sem(f"att_w_in{i}") for i in range(4)]
        att_w_hi = sem("att_w_hi")
        att_w_ready = sem("att_w_ready")
        att_vo_ready = sem("att_vo_ready")
        mix_full = sem("mix_full")
        mix_hi_ready = sem("mix_hi_ready")
        mix_ready = sem("mix_ready")

        fw_buf = [x[:, 8:12, :], x[:, 12:16, :]]
        fw_tmp = x[:, 4:8, :]
        fw_parts = [(xT_hi[:, 3, :, :], xT_lo[:, 3, :, :]), (v_hi, v_lo)]
        stage = [hid[0], hid[1], xn[0], xn[1]]
        had_raw = half_down_s[:, 0:P]
        had = hid_hi[0][:, 0:P]
        neg_had = hid_hi[0][:, P:2 * P]
        att_raw = [nc.alloc_sbuf_tensor_at(f"att_raw{i}", [P, KD, D], F32, offset=mix_at + 16 * D * at)[:, :, :]
                   for i, at in enumerate((0, 2, 1, 3))]
        att_at = [1, 2, 1, 2]

        def added_no(li, tile):
            before = TT * CH * len(SIZES["B"]) if li == LAST else 0
            return tile - tile_no[li, 0, 0] + before

        block = ctx.enter_context(nc.Block())

        def three(pe, out, a_hi, a_lo, b_hi, b_lo, start, stop, zero=None):
            pe.matmul(out, a_hi, b_hi, start=start, stop=False)
            if zero != "b":
                last = pe.matmul(out, a_hi, b_lo, start=False, stop=stop and zero == "a")
            if zero != "a":
                last = pe.matmul(out, a_lo, b_hi, start=False, stop=stop)
            return last

        @block.sync
        def _(sp):
            sp.dma_start(had_raw, t["hadamard"]).then_inc(had_in, 16)
            for i in (0, 1):
                sp.dma_start(att_raw[i], t["att_w"][i]).then_inc(att_w_in[i], 16)

            def slice_in(s):
                sp.dma_start(fw_buf[s % 2].rearrange("p a (b d) -> p (a b) d", b=4),
                             t["w2a"][s]).then_inc(fw_in[s], 16)

            slice_in(0)
            slice_in(1)
            sp.dma_start(ident[:, :], t["ident"]).then_inc(consts_in, 16)
            sp.dma_start(causal[:, :], t["causal"]).then_inc(consts_in, 16)
            sp.dma_start(small[:, :], t["small"]).then_inc(consts_in, 16)
            sp.dma_start(x[:, 0:TT, :], t["x"][:, 0:TT, :]).then_inc(x_in[0], 16)
            sp.wait_ge(fw_ready, 1)
            slice_in(2)
            for i in (2, 3):
                sp.dma_start(att_raw[i], t["att_w"][i]).then_inc(att_w_in[i], 16)
            sp.wait_ge(fw_ready, 2)
            slice_in(3)
            for part, name in ((0, "w1a"), (1, "w3a")):
                sp.dma_start(raw[:, part, :].rearrange("p (b n) -> p b n", b=2),
                             t[name][0:2, :, :].rearrange("b p n -> p b n")).then_inc(first_in, 16)
            sp.wait_ge(fly_ready, 4)
            sp.dma_start(x[:, TT:2 * TT, :], t["x"][:, TT:2 * TT, :]).then_inc(x_in[1], 16)
            for c in (2, 3):
                sp.wait_ge(fw_ready, c + 1)
                sp.dma_start(x[:, c * TT:(c + 1) * TT, :], t["x"][:, c * TT:(c + 1) * TT, :]
                             ).then_inc(x_in[c], 16)

            def load(src, b0, size, parts=(0, 1, 2)):
                for part in parts:
                    sp.dma_start(
                        raw[:, part, 0:size * D].rearrange("p (b n) -> p b n", b=size),
                        src[part][bass.ds(b0, size), :, :].rearrange("b p n -> p b n")
                    ).then_inc(raw_in, 16)

            sources = {"A": (t["w1a"], t["w3a"], w2_scratch), "B": (t["gate"], t["up"], t["down"]),
                       "S": (t["b"], None, t["c"])}
            for j in range(4):
                sp.wait_ge(scratch_done[j], 64)
            for li, kind in enumerate(LAYERS):
                b0 = 0
                if kind == "B" and li < LAST:
                    sp.wait_ge(acc_free, tile_no[1, CH - 1] + TT)
                    sp.dma_start(skip_d[:, :], t["skip_d"]).then_inc(skip_in, 16)
                    sp.dma_start(half_down_s[:, :], t["down_s"]).then_inc(down_s_in, 16)
                for g, size in enumerate(SIZES[kind]):
                    if kind == "A" and g:
                        break
                    if li or g:
                        before = previous(li, g) or (0, len(SIZES["A"]) - 1)
                        sp.wait_ge(w_ready, parts_no[before])
                        load(sources[kind], b0, size, (0, 2) if kind == "S" else (0, 1, 2))
                    else:
                        load(sources[kind], b0, size, (2,))
                    b0 += size
                if kind == "A":
                    with sp.Fori(1, len(SIZES["A"])) as g:
                        sp.wait_ge(w_ready, (parts_no[li, 0] - 3) + g * 3)
                        load(sources[kind], g * 2, 2)
            for c in range(CH):
                sp.wait_ge(x_added, added_no(LAST, tile_no[LAST, len(SIZES["B"]) - 1, c]) + TT)
                sp.dma_start(t["out"][:, c * TT:(c + 1) * TT, :],
                             x[:, c * TT:(c + 1) * TT, :]).then_inc(out_done, 16)
            sp.wait_ge(out_done, 16 * CH)

        @block.tensor
        def _(pe):
            def mix(m, ready, n):
                pe.wait_ge(ready, n)
                a, b = att_at[2 * m], att_at[2 * m + 1]
                for k in range(KD):
                    if m:
                        pe.wait_ge(fw_out, 8 + k + 1)
                    for j in range(KD):
                        last = three(pe, (acc if m else work)[:, k, :],
                                     xT_hi[:, a, j, k * P:(k + 1) * P], xT_lo[:, a, j, k * P:(k + 1) * P],
                                     xT_hi[:, b, j, :], xT_lo[:, b, j, :], j == 0, j == KD - 1)
                    last.then_inc(mix_full, 1)

            mix(0, att_w_ready, 2)
            pe.wait_ge(had_ready, 2)
            for s in range(4):
                pe.wait_ge(fw_ready, s + 1)
                hi, lo = fw_parts[s % 2]
                banks = work if s % 2 else acc
                for j in range(4):
                    if s == 1:
                        pe.wait_ge(mix_ready, j + 1)
                    if s >= 2:
                        pe.wait_ge(fw_out, 4 * (s - 2) + j + 1)
                    for i in range(4):
                        sign = neg_had if bin(i & j).count("1") % 2 else had
                        pe.matmul(banks[:, j, :], sign, hi[:, i, :], start=i == 0, stop=False)
                        last = pe.matmul(banks[:, j, :], sign, lo[:, i, :], start=False, stop=i == 3)
                    last.then_inc(fw_full, 1)
            mix(1, att_vo_ready, 2)
            pe.wait_ge(fw_out, 16)

            xn_pairs = [0]

            def pair_wait(w):
                if isinstance(w, int) and w < 2:
                    return
                pe.wait_ge(pair_free, w - 1)

            def transpose_pair(key):
                w = use[key]
                pair_wait(w)
                xn_pairs[0] += 1
                pe.wait_ge(xn_ready, 2 * xn_pairs[0])
                for j in range(2):
                    for k in range(KD):
                        last = pe.transpose(work[:, w % 2 * 2 + j, k * P:(k + 1) * P],
                                            xn[j][:, k * P:(k + 1) * P], ident[:, :])
                last.then_inc(pair_full, 1)

            def up(w, pair, c, buf, b, matrices, exact=False):
                pair_wait(w)
                for m in range(matrices):
                    for k in range(KD):
                        at = slice(b * D + k * P, b * D + (k + 1) * P)
                        last = three(pe, work[:, 2 * pair + m, :], w_hi[buf][:, m, at], w_lo[buf][:, m, at],
                                     xT_hi[:, c, k, :], xT_lo[:, c, k, :], k == 0, k == KD - 1,
                                     "a" if exact else None)
                last.then_inc(pair_full, 1)

            def down(n, h, buf, b, size, tile, exact=False):
                pe.wait_ge(hid_lo_ready, n + 1)
                at = slice(b * D, (b + 1) * D)
                for i in range(TT):
                    if b == 0 and not (isinstance(tile, int) and tile < TT):
                        pe.wait_ge(acc_free, tile - 3 + i)
                    ts = slice(i * P, (i + 1) * P)
                    last = three(pe, acc[:, i, :], hid_hi[h][:, ts], hid_lo[h][:, ts],
                                 w_hi[buf][:, 2, at], w_lo[buf][:, 2, at], b == 0, b == size - 1,
                                 "b" if exact else None)
                    if b == size - 1:
                        last.then_inc(acc_ready, 1)

            def both_ways(flag, emit):
                at = xn_pairs[0]
                with pe.If(flag == 0):
                    emit(True)
                xn_pairs[0] = at
                with pe.Else():
                    emit(False)

            flags = {}

            def down_before(li, g, c0, d, dt, exact):
                n = block_no[li, g, c0, 0] - 1
                tile = tile_no[li, g, c0] - TT + dt
                if c0:
                    size = SIZES[LAYERS[li]][g]
                    down(n + d, n % 2, group_buffer(li, g), size - 1, size, tile, exact)
                elif previous(li, g):
                    lp, gp = previous(li, g)
                    size = SIZES[LAYERS[lp]][gp]
                    emit = lambda e: down(n + d, n % 2, group_buffer(lp, gp), size - 1, size, tile, e)
                    if (lp, gp) in flags:
                        both_ways(flags[lp, gp], emit)
                    else:
                        emit(False)

            def up_block(li, g, c0, c, b, d, exact):
                w = use[li, g, c0, b]
                up(w + d, w % 2, c, group_buffer(li, g), b, 1 if LAYERS[li] == "S" else 2, exact)

            def rest(li, g, c0, c, d, dt, exact):
                size, buf = SIZES[LAYERS[li]][g], group_buffer(li, g)
                for b in range(size):
                    if b:
                        up_block(li, g, c0, c, b, d, exact)
                        n = block_no[li, g, c0, b] - 1
                        down(n + d, n % 2, buf, b - 1, size, tile_no[li, g, c0] + dt, exact)
                    if (li, g, c0, b) in plan.after:
                        transpose_pair(plan.after[li, g, c0, b])

            def other_steps(li, g, d, dt, exact):
                if g in (0, len(SIZES[LAYERS[li]]) - 1) or SIZES[LAYERS[li]][g] == 1:
                    for c in range(1, CH):
                        if g == 0:
                            pe.wait_ge(pair_free, use["x", li, c, 1] + 1)
                        up_block(li, g, c, c, 0, d, exact)
                        down_before(li, g, c, d, dt, exact)
                        rest(li, g, c, c, d, dt, exact)
                else:
                    with pe.Fori(0, CH - 1) as e:
                        de, dte = e * 2 + d, e * TT + dt
                        up_block(li, g, 1, e + 1, 0, de, exact)
                        down_before(li, g, 1, de, dte, exact)
                        rest(li, g, 1, e + 1, de, dte, exact)

            def group(li, g, d=0, dt=0, dp=0):
                pe.wait_ge(w_ready, parts_no[li, g] + dp)
                if g == 0:
                    pe.wait_ge(pair_free, use["x", li, 0, 1] + 1)
                if LAYERS[li] != "B":
                    up_block(li, g, 0, 0, 0, d, False)
                    down_before(li, g, 0, d, dt, False)
                    rest(li, g, 0, 0, d, dt, False)
                    other_steps(li, g, d, dt, False)
                    return
                pe.wait_ge(flag_ready, g + 1)
                flag = flags[li, g] = pe.value_load(inexact[0:1, g:g + 1], min_val=0, max_val=LOW_BITS)
                both_ways(flag, lambda exact: up_block(li, g, 0, 0, 0, d, exact))
                down_before(li, g, 0, d, dt, False)

                def remaining(exact):
                    rest(li, g, 0, 0, d, dt, exact)
                    other_steps(li, g, d, dt, exact)

                both_ways(flag, remaining)

            def q_pair(c, j):
                w = use["q", c, j]
                pair_wait(w)
                for i in range(2):
                    m = slice((2 * j + i) * P, (2 * j + i + 1) * P)
                    for k in range(KD):
                        last = three(pe, work[:, w % 2 * 2 + i, :], mix_hi[:, 0, k, m], mix_lo[:, 0, k, m],
                                     xT_hi[:, c, k, :], xT_lo[:, c, k, :], k == 0, k == KD - 1)
                last.then_inc(pair_full, 1)

            def v_pair(c, j):
                w = use["v", c, j]
                pair_wait(w)
                for i in range(2):
                    m = slice((2 * j + i) * P, (2 * j + i + 1) * P)
                    for k in range(KD):
                        last = three(pe, work[:, w % 2 * 2 + i, :], xT_hi[:, c, k, m], xT_lo[:, c, k, m],
                                     mix_hi[:, 1, k, :], mix_lo[:, 1, k, :], k == 0, k == KD - 1)
                last.then_inc(pair_full, 1)

            def scores(c, i):
                pe.wait_ge(acc_free, tile_no[1, c] - 3 + i)
                n = (i + 1) * P
                for k in range(KD):
                    last = three(pe, acc[:, i, 0:n], qT_hi[:, k, i * P:n], qT_lo[:, k, i * P:n],
                                 xT_hi[:, c, k, 0:n], xT_lo[:, c, k, 0:n], k == 0, k == KD - 1)
                last.then_inc(score_ready, 1)

            def p_transpose(c, i):
                w = use["p", c, i]
                pair_wait(w)
                pe.wait_ge(exp_ready, TT * c + i + 1)
                for k in range(i + 1):
                    last = pe.transpose(work[:, w % 2 * 2, k * P:(k + 1) * P],
                                        hid[i % 2][:, k * P:(k + 1) * P], ident[:, :])
                last.then_inc(pair_full, 1)

            def attend(c, i):
                pe.wait_ge(pair_free, use["p", c, i] + 1)
                for k in range(i + 1):
                    ks = slice(k * P, (k + 1) * P)
                    last = three(pe, acc[:, i, :], hid_hi[i % 2][:, ks], hid_lo[i % 2][:, ks],
                                 v_hi[:, k, :], v_lo[:, k, :], k == 0, k == i)
                last.then_inc(acc_ready, 1)

            def attention(li):
                pe.wait_ge(pair_free, use["x", li, 0, 1] + 1)
                q_pair(0, 0)
                lp, gp = li - 1, len(SIZES[LAYERS[li - 1]]) - 1
                n = block_no[lp, gp, CH - 1, 1]
                down(n, n % 2, group_buffer(lp, gp), 1, 2, tile_no[lp, gp, CH - 1])
                q_pair(0, 1)
                for c in range(CH):
                    more = c + 1 < CH
                    first = ("x", 1, c + 2) if c < 2 else ("x", 2, c - 1)
                    pe.wait_ge(pair_free, use["q", c, 1] + 1)
                    for i in range(TT):
                        scores(c, i)
                    v_pair(c, 0)
                    p_transpose(c, 0)
                    v_pair(c, 1)
                    transpose_pair(first + (0,))
                    p_transpose(c, 1)
                    if more:
                        pe.wait_ge(pair_free, use["x", li, c + 1, 1] + 1)
                        q_pair(c + 1, 0)
                    attend(c, 0)
                    p_transpose(c, 2)
                    transpose_pair(first + (1,))
                    if more:
                        q_pair(c + 1, 1)
                    attend(c, 1)
                    p_transpose(c, 3)
                    if c == 1:
                        transpose_pair(("x", 2, 0, 0))
                    attend(c, 2)
                    if c == 1:
                        transpose_pair(("x", 2, 0, 1))
                    attend(c, 3)

            pe.wait_ge(consts_in, 48)
            for c in (0, 1):
                for half in (0, 1):
                    transpose_pair(("x", 0, c, half))
            pe.wait_ge(mix_ready, 2 * KD)
            for li, kind in enumerate(LAYERS):
                G = len(SIZES[kind])
                if kind == "T":
                    attention(li)
                elif kind == "A":
                    group(li, 0)
                    with pe.Fori(0, (G - 2) // 2) as o:
                        group(li, 1, o * 16, o * 32, o * 6)
                        group(li, 2, o * 16, o * 32, o * 6)
                    group(li, G - 1)
                else:
                    for g in range(G):
                        group(li, g)
            g = len(SIZES["B"]) - 1
            n = block_no[LAST, g, CH - 1, 1]
            both_ways(flags[LAST, g], lambda exact: down(n, n % 2, group_buffer(LAST, g), 1, 2,
                                                         tile_no[LAST, g, CH - 1], exact))

        @block.scalar
        def _(act):
            act.wait_ge(had_in, 16)
            nc.scalar.activation(had, had_raw, ACT.Copy).then_inc(had_ready, 1)
            nc.scalar.activation(neg_had, had_raw, ACT.Copy, scale=-1.0).then_inc(had_ready, 1)

            def fw_split(s):
                act.wait_ge(fly_ready, s + 1)
                nc.scalar.activation(fw_parts[s % 2][0], fw_buf[s % 2], ACT.Copy).then_inc(fw_hi_ready, 1)

            def fw_scale(s):
                for j in range(4):
                    act.wait_ge(fw_full, 4 * s + j + 1)
                    if s:
                        act.wait_ge(scratch_done[j], 16 * s)
                    nc.scalar.activation(stage[j][:, :], (work if s % 2 else acc)[:, j, :], ACT.Copy,
                                         scale=0.5 * HA ** -0.5).then_inc(fw_out, 1)
                    act.wait_ge(fw_out, 4 * s + j + 1)
                    act.dma_start(
                        w2_scratch[4 * j:4 * j + 4, :, s * P:(s + 1) * P].rearrange("b p d -> p b d"),
                        stage[j][:, :].rearrange("p (b d) -> p b d", b=4)).then_inc(scratch_done[j], 16)

            def att_split(i):
                act.wait_ge(att_w_in[i], 16)
                nc.scalar.activation(xT_hi[:, att_at[i], :, :], att_raw[i], ACT.Copy).then_inc(att_w_hi, 1)

            def mix_split(m):
                for k in range(KD):
                    act.wait_ge(mix_full, KD * m + k + 1)
                    nc.scalar.activation(mix_hi[:, m, k, :], (acc if m else work)[:, k, :],
                                         ACT.Copy).then_inc(mix_hi_ready, 1)

            att_split(0)
            att_split(1)
            fw_split(0)
            fw_split(1)
            act.wait_ge(att_w_ready, 2)
            mix_split(0)
            fw_scale(0)
            fw_split(2)
            att_split(2)
            att_split(3)
            fw_scale(1)
            fw_split(3)
            fw_scale(2)
            act.wait_ge(first_in, 32)
            for part in (0, 1):
                nc.scalar.activation(w_hi[0][:, part, :], raw[:, part, :], ACT.Copy).then_inc(w_hi_ready, 1)
            fw_scale(3)
            act.wait_ge(att_vo_ready, 2)
            mix_split(1)

            affine_pairs = [0]
            w_parts = [0]

            def split_part(li, g, part, prepared=0):
                size, buf = SIZES[LAYERS[li]][g], group_buffer(li, g)
                nc.scalar.activation(w_hi[buf][:, part, 0:size * D], raw[:, part, 0:size * D],
                                     ACT.Copy).then_inc(w_hi_ready, 1)

            def weights_here(li, g, dr=0):
                act.wait_ge(raw_in, raw_count[li, g] + dr)

            def up(w, pair, n, h, li, blk):
                act.wait_ge(pair_full, w + 1)
                if LAYERS[li] == "S":
                    nc.scalar.activation(hid[h][:, :], work[:, 2 * pair, :], ACT.Tanh).then_inc(act_ready, 1)
                    return
                scale = gate_s[:, blk:blk + 1] if LAYERS[li] == "B" else 1.0
                nc.scalar.activation(hid[h][:, :], work[:, 2 * pair, :], ACT.Silu,
                                     scale=scale).then_inc(act_ready, 1)
                act.wait_ge(pair_free, w + 1)
                nc.scalar.activation(hid_hi[h][:, :], hid[h][:, :], ACT.Copy).then_inc(hid_hi_ready, 1)

            def transpose_pair(key):
                w = use[key]
                act.wait_ge(pair_full, w + 1)
                if LAYERS[key[1]] == "T":
                    affine_pairs[0] += 1
                    act.wait_ge(affine_ready, affine_pairs[0])
                for j in range(2):
                    ts = slice((2 * key[3] + j) * P, (2 * key[3] + j + 1) * P)
                    nc.scalar.activation(
                        xT_hi[:, key[2], :, ts],
                        work[:, w % 2 * 2 + j, :].rearrange("p (k t) -> p k t", k=KD),
                        ACT.Copy).then_inc(xT_hi_ready, 1)

            def step(li, g, c0, c, d=0, dr=0):
                for b in range(SIZES[LAYERS[li]][g]):
                    w, n = use[li, g, c0, b], block_no[li, g, c0, b]
                    up(w + d, w % 2, n + d, n % 2, li, sum(SIZES[LAYERS[li]][:g]) + b)
                    if c0 and b == 0 and following(li, g):
                        ln, gn = following(li, g)
                        if not isinstance(c, int):
                            if c0 == 1:
                                weights_here(ln, gn, dr)
                            split_part(ln, gn, c - 1)
                        elif not (LAYERS[ln] == "S" and c == 2):
                            weights_here(ln, gn, dr)
                            split_part(ln, gn, c - 1)
                    if (li, g, c0, b) in plan.after:
                        transpose_pair(plan.after[li, g, c0, b])

            def group(li, g, d=0, dr=0):
                step(li, g, 0, 0, d, dr)
                G = len(SIZES[LAYERS[li]])
                if g in (0, G - 1) or SIZES[LAYERS[li]][g] == 1:
                    for c in range(1, CH):
                        step(li, g, c, c, d, dr)
                else:
                    with act.Fori(0, CH - 1) as e:
                        step(li, g, 1, e + 1, e * 2 + d, dr)

            def pair_hi(key, dst):
                w = use[key]
                act.wait_ge(pair_full, w + 1)
                for i in range(2):
                    nc.scalar.activation(dst[:, 2 * key[2] + i, :], work[:, w % 2 * 2 + i, :],
                                         ACT.Copy).then_inc(att_hi_ready, 1)

            def numerators(c, i):
                act.wait_ge(max_ready, TT * c + i + 1)
                if i >= 2:
                    act.wait_ge(pair_full, use["p", c, i - 2] + 1)
                n = (i + 1) * P
                nc.scalar.activation(hid[i % 2][:, 0:n], acc[:, i, 0:n], ACT.Exp,
                                     bias=negmax[:, i:i + 1], scale=SCORE_SCALE,
                                     accum_out=rowsum[:, i:i + 1]).then_inc(exp_ready, 1)

            def p_hi(c, i):
                w = use["p", c, i]
                act.wait_ge(pair_full, w + 1)
                if i >= 2:
                    act.wait_ge(acc_ready, tile_no[1, c] + i - 1)
                n = (i + 1) * P
                nc.scalar.activation(hid_hi[i % 2][:, 0:n], work[:, w % 2 * 2, 0:n],
                                     ACT.Copy).then_inc(att_hi_ready, 1)

            def attention(li):
                for j in range(2):
                    pair_hi(("q", 0, j), qT_hi)
                for c in range(CH):
                    more = c + 1 < CH
                    first = ("x", 1, c + 2) if c < 2 else ("x", 2, c - 1)
                    numerators(c, 0)
                    numerators(c, 1)
                    pair_hi(("v", c, 0), v_hi)
                    p_hi(c, 0)
                    pair_hi(("v", c, 1), v_hi)
                    transpose_pair(first + (0,))
                    p_hi(c, 1)
                    numerators(c, 2)
                    if more:
                        pair_hi(("q", c + 1, 0), qT_hi)
                    numerators(c, 3)
                    p_hi(c, 2)
                    transpose_pair(first + (1,))
                    if more:
                        pair_hi(("q", c + 1, 1), qT_hi)
                    else:
                        weights_here(li + 1, 0)
                        for part in range(3):
                            split_part(li + 1, 0, part)
                    p_hi(c, 3)
                    if c == 1:
                        transpose_pair(("x", 2, 0, 0))
                        transpose_pair(("x", 2, 0, 1))

            for half in (0, 1):
                transpose_pair(("x", 0, 0, half))
            weights_here(0, 0)
            split_part(0, 0, 2)
            for half in (0, 1):
                transpose_pair(("x", 0, 1, half))
            for j in (0, 1):
                act.wait_ge(scratch_done[j], 64)
            for li, kind in enumerate(LAYERS):
                G = len(SIZES[kind])
                if kind == "T":
                    attention(li)
                elif kind == "A":
                    group(li, 0)
                    with act.Fori(0, (G - 2) // 2) as o:
                        group(li, 1, o * 16, o * 96)
                        group(li, 2, o * 16, o * 96)
                    group(li, G - 1)
                else:
                    for g in range(G):
                        group(li, g)

        @block.gpsimd
        def _(pool):
            pool.memset(minus_half[:, :], -0.5).then_inc(pool_step, 1)
            steps = [1]

            def deviation(out, var, n):
                pool.tensor_scalar(var_eps[:, 0:n], var, 1.0, EPS, ALU.mult, ALU.add).then_inc(pool_step, 1)
                steps[0] += 1
                pool.wait_ge(pool_step, steps[0])
                return pool.tensor_tensor(out, var_eps[:, 0:n], minus_half[:, 0:n], ALU.pow)

            done, done2 = [0], [0]

            def var_eps_read():
                if done[0]:
                    pool.wait_ge(rstd_ready, done[0])
                if done2[0]:
                    pool.wait_ge(rstd2_ready, done2[0])

            def chunk(c):
                var_eps_read()
                done[0] += 1
                pool.wait_ge(stats_ready, done[0])
                deviation(rstd[:, c * TT:(c + 1) * TT], meanvar[:, c * TT:(c + 1) * TT, 1], TT
                          ).then_inc(rstd_ready, 1)

            def second():
                var_eps_read()
                done2[0] += 1
                pool.wait_ge(stats2_ready, done2[0])
                deviation(rstd2[:, :], meanvar2[:, :, 1], 2).then_inc(rstd2_ready, 1)

            def flag(g):
                pool.wait_ge(low_ready, g + 1)
                pool.partition_all_reduce(inexact[:, g:g + 1], low_max[:, g:g + 1], P, MAX
                                          ).then_inc(flag_ready, 1)

            def add_tiles(tile, c):
                for i in range(TT):
                    pool.wait_ge(acc_free, tile + i + 1)
                    pool.tensor_tensor(x[:, c * TT + i, :], x[:, c * TT + i, :], scaled[:, i, :],
                                       ALU.add).then_inc(x_added, 1)

            def ffn_b(li):
                G = len(SIZES["B"])
                for g in range(G):
                    if g:
                        add_tiles(tile_no[li, g - 1, CH - 1], CH - 1)
                    if g + 1 < G and li < LAST:
                        flag(g + 1)
                    if g == G - 1:
                        for c in range(CH - 1):
                            add_tiles(tile_no[li, g, c], c)
                            if li < LAST:
                                chunk(c)
                    else:
                        with pool.Fori(0, CH - 1) as e:
                            add_tiles(e * TT + tile_no[li, g, 0], e)
                add_tiles(tile_no[li, G - 1, CH - 1], CH - 1)
                if li < LAST:
                    chunk(CH - 1)

            for i in (2, 3):
                pool.wait_ge(att_w_hi, i + 1)
                pool.tensor_tensor(xT_lo[:, att_at[i], :, :], att_raw[i], xT_hi[:, att_at[i], :, :],
                                   ALU.subtract).then_inc(att_vo_ready, 1)
            for c in range(CH):
                chunk(c)
            for li in range(1, LAST + 1):
                if LAYERS[li - 1] == "B":
                    ffn_b(li - 1)
                    continue
                if LAYERS[li] == "B" and li < LAST:
                    flag(0)
                if LAYERS[li] != "T":
                    for c in range(CH if LAYERS[li - 1] != "T" else 1):
                        chunk(c)
                    if LAYERS[li - 1] == "T":
                        second()
                        second()
                        for c in range(1, CH):
                            chunk(c)
                else:
                    chunk(0)
                    second()
                    for c in range(1, CH):
                        chunk(c)
                        second()
                        if c < CH - 1:
                            second()
            ffn_b(LAST)

        @block.vector
        def _(dve):
            steps = [0]

            def link(ins):
                steps[0] += 1
                ins.then_inc(dve_step, 1)
                dve.wait_ge(dve_step, steps[0])

            chunks = [0]

            def norm_stats(li, c, first=False):
                if chunks[0]:
                    dve.wait_ge(stats_ready, chunks[0])
                chunks[0] += 1
                if first:
                    dve.wait_ge(x_in[c], 16)
                for i in range(TT):
                    last = nc.vector.bn_stats(stats[:, i, :], x[:, c * TT + i, :])
                link(last)
                for i in range(TT):
                    last = nc.vector.bn_aggr(meanvar[:, c * TT + i, :], stats[:, i, :])
                last.then_inc(stats_ready, 1)

            def fly(dst, src, pattern):
                s = src.rearrange("p a (b d) -> p a b d", b=4)
                o = dst.rearrange("p a (b d) -> p a b d", b=4)
                if pattern == 0:
                    lo_s, hi_s, lo_o, hi_o = s[:, :, 0:4:2, :], s[:, :, 1:4:2, :], o[:, :, 0:4:2, :], o[:, :, 1:4:2, :]
                else:
                    lo_s, hi_s, lo_o, hi_o = s[:, :, 0:2, :], s[:, :, 2:4, :], o[:, :, 0:2, :], o[:, :, 2:4, :]
                nc.vector.tensor_tensor(lo_o, lo_s, hi_s, ALU.add)
                return nc.vector.tensor_tensor(hi_o, lo_s, hi_s, ALU.subtract)

            def fw_slice(s):
                buf = fw_buf[s % 2]
                dve.wait_ge(fw_in[s], 16)
                if s:
                    dve.wait_ge(fly_ready, s)
                link(fly(fw_tmp, buf, 0))
                fly(buf, fw_tmp, 1).then_inc(fly_ready, 1)
                dve.wait_ge(fw_hi_ready, s + 1)
                nc.vector.tensor_tensor(fw_parts[s % 2][1], buf, fw_parts[s % 2][0],
                                        ALU.subtract).then_inc(fw_ready, 1)

            def mix_split(m):
                for k in range(KD):
                    dve.wait_ge(mix_hi_ready, KD * m + k + 1)
                    nc.vector.tensor_tensor(mix_lo[:, m, k, :], (acc if m else work)[:, k, :],
                                            mix_hi[:, m, k, :], ALU.subtract).then_inc(mix_ready, 1)

            for i in (0, 1):
                dve.wait_ge(att_w_hi, i + 1)
                nc.vector.tensor_tensor(xT_lo[:, att_at[i], :, :], att_raw[i],
                                        xT_hi[:, att_at[i], :, :], ALU.subtract).then_inc(att_w_ready, 1)
            fw_slice(0)
            fw_slice(1)
            mix_split(0)
            fw_slice(2)
            fw_slice(3)
            norm_stats(0, 0, True)
            norm_stats(0, 1, True)

            normed, normed2, hi_tiles, att_his, w_part, rstds = [0], [0], [0], [0], [0], {}

            def normalise(key):
                _, li, c, half = key
                dve.wait_ge(rstd_ready, 4 * li + c + 1)
                kind = LAYERS[li]
                for j in range(2):
                    i = c * TT + 2 * half + j
                    last = nc.vector.tensor_scalar(xn[j][:, :], x[:, i, :], meanvar[:, i, 0:1], rstd[:, i:i + 1],
                                                   ALU.subtract, ALU.mult)
                    if kind != "T" and kind != "S":
                        last.then_inc(xn_ready, 1)
                if kind == "T":
                    link(last)
                    if normed2[0]:
                        dve.wait_ge(stats2_ready, normed2[0])
                    for j in range(2):
                        last = nc.vector.bn_stats(stats2[:, j, :], xn[j][:, :])
                    link(last)
                    for j in range(2):
                        last = nc.vector.bn_aggr(meanvar2[:, j, :], stats2[:, j, :])
                    last.then_inc(stats2_ready, 1)
                    for j in range(2):
                        i = c * TT + 2 * half + j
                        last = nc.vector.tensor_tensor(x[:, i, :], x[:, i, :], xn[j][:, :], ALU.add)
                    link(last)
                    normed2[0] += 1
                    dve.wait_ge(rstd2_ready, normed2[0])
                    for j in range(2):
                        nc.vector.tensor_scalar(xn[j][:, :], xn[j][:, :], meanvar2[:, j, 0:1], rstd2[:, j:j + 1],
                                                ALU.subtract, ALU.mult).then_inc(xn_ready, 1)
                if kind == "S":
                    link(last)
                    dve.wait_ge(skip_in, 16)
                    for j in range(2):
                        i = c * TT + 2 * half + j
                        link(nc.vector.tensor_tensor(skip_t, xn[j][:, :], skip_d[:, :], ALU.mult))
                        nc.vector.tensor_tensor(x[:, i, :], x[:, i, :], skip_t, ALU.add).then_inc(xn_ready, 1)
                        dve.wait_ge(xn_ready, 2 * normed[0] + j + 1)
                normed[0] += 1

            def transpose_pair(key):
                w = use[key]
                if LAYERS[key[1]] == "T":
                    dve.wait_ge(pair_full, w + 1)
                    for k in range(KD):
                        bank = work[:, w % 2 * 2:w % 2 * 2 + 2, k * P:(k + 1) * P]
                        last = nc.vector.tensor_scalar(bank, bank, gamma[:, k:k + 1], beta[:, k:k + 1],
                                                       ALU.mult, ALU.add)
                    last.then_inc(affine_ready, 1)
                for j in range(2):
                    hi_tiles[0] += 1
                    dve.wait_ge(xT_hi_ready, hi_tiles[0])
                    ts = slice((2 * key[3] + j) * P, (2 * key[3] + j + 1) * P)
                    last = nc.vector.tensor_tensor(
                        xT_lo[:, key[2], :, ts],
                        work[:, w % 2 * 2 + j, :].rearrange("p (k t) -> p k t", k=KD),
                        xT_hi[:, key[2], :, ts], ALU.subtract)
                last.then_inc(pair_free, 1)

            def up(w, pair, n, n_ffn, h, li, blk):
                dve.wait_ge(act_ready, n + 1)
                if LAYERS[li] == "S":
                    nc.vector.tensor_copy(hid_hi[h][:, :], hid[h][:, :]).then_inc(pair_free, 1)
                    dve.wait_ge(pair_free, w + 1)
                else:
                    scale = up_s[:, blk:blk + 1] if LAYERS[li] == "B" else 1.0
                    nc.vector.scalar_tensor_tensor(hid[h][:, :], work[:, 2 * pair + 1, :], scale, hid[h][:, :],
                                                   ALU.mult, ALU.mult).then_inc(pair_free, 1)
                    dve.wait_ge(hid_hi_ready, n_ffn + 1)
                nc.vector.tensor_tensor(hid_lo[h][:, :], hid[h][:, :], hid_hi[h][:, :],
                                        ALU.subtract).then_inc(hid_lo_ready, 1)

            def add_tiles(li, tile, c):
                for i in range(TT):
                    dve.wait_ge(acc_ready, tile + i + 1)
                    if LAYERS[li] == "B":
                        added = added_no(li, tile) - TT + i + 1
                        if not isinstance(added, int) or added > 0:
                            dve.wait_ge(x_added, added)
                        nc.vector.tensor_tensor(scaled[:, i, :], acc[:, i, :], half_down_s[:, :],
                                                ALU.mult).then_inc(acc_free, 1)
                        continue
                    nc.vector.tensor_tensor(x[:, c * TT + i, :], acc[:, i, :], x[:, c * TT + i, :],
                                            ALU.add).then_inc(acc_free, 1)

            def split_part(li, g, part, no):
                size, buf = SIZES[LAYERS[li]][g], group_buffer(li, g)
                dve.wait_ge(w_hi_ready, no)
                nc.vector.tensor_tensor(w_lo[buf][:, part, 0:size * D], raw[:, part, 0:size * D],
                                        w_hi[buf][:, part, 0:size * D], ALU.subtract).then_inc(w_ready, 1)

            def find_low_bits(li, g):
                dve.wait_ge(raw_in, raw_count[li, g])
                if g:
                    dve.wait_ge(low_ready, g)
                n = SIZES[LAYERS[li]][g] * D
                link(nc.vector.tensor_scalar(low_bits[:, :, 0:n], raw[:, :, 0:n].bitcast(U32), LOW_BITS, None,
                                             ALU.bitwise_and))
                nc.vector.tensor_reduce(low_max[:, g:g + 1], low_bits[:, :, 0:n], AX.XY,
                                        ALU.max).then_inc(low_ready, 1)

            def finish_chunk(li, g, c):
                if li < LAST and g == len(SIZES[LAYERS[li]]) - 1:
                    if LAYERS[li] == "B":
                        dve.wait_ge(x_added, added_no(li, tile_no[li, g, c]) + TT)
                    else:
                        dve.wait_ge(acc_free, tile_no[li, g, c] + TT)
                    norm_stats(li + 1, c)

            def step(li, g, c0, c, d=0, dt=0, dp=0, inner=0):
                kind = LAYERS[li]
                for b in range(SIZES[kind][g]):
                    w, n = use[li, g, c0, b], block_no[li, g, c0, b]
                    ffn_before = sum(SIZES["S"]) * CH if li > LAYERS.index("S") else 0
                    up(w + d, w % 2, n + d, n - ffn_before + d, n % 2, li, sum(SIZES[kind][:g]) + b)
                    if b == 0 and c0:
                        add_tiles(li, tile_no[li, g, c0] - TT + dt, c - 1)
                        if isinstance(c, int):
                            finish_chunk(li, g, c - 1)
                    elif b == 0 and previous(li, g):
                        add_tiles(previous(li, g)[0], tile_no[li, g, c0] - TT + dt, CH - 1)
                        if isinstance(c, int) and g == 0:
                            finish_chunk(*previous(li, g), CH - 1)
                    if b == 0 and following(li, g):
                        ln, gn = following(li, g)
                        base = parts_no[ln, gn] - (2 if LAYERS[ln] == "S" else 3)
                        if c0 == 0:
                            if ln == LAYERS.index("B"):
                                find_low_bits(ln, gn)
                        elif LAYERS[ln] != "S":
                            split_part(ln, gn, c - 1, base + c + dp)
                        elif c != 2:
                            split_part(ln, gn, c - 1, base + (c + 1) // 2)
                    if (li, g, c0, b) in plan.after:
                        key = plan.after[li, g, c0, b]
                        transpose_pair(key)
                        if key[3] == 0:
                            normalise(key[:3] + (1,))
                if isinstance(c, int) and c and g == len(SIZES[kind]) - 1 and li < LAST:
                    normalise(("x", li + 1, c - 1, 0))
                if g == 0 and c0 == 0:
                    normalise(("x", li, CH - 1, 0))

            def group(li, g, d=0, dt=0, dp=0):
                step(li, g, 0, 0, d, dt, dp)
                G = len(SIZES[LAYERS[li]])
                if g in (0, G - 1) or SIZES[LAYERS[li]][g] == 1:
                    for c in range(1, CH):
                        step(li, g, c, c, d, dt, dp)
                else:
                    with dve.Fori(0, CH - 1) as e:
                        step(li, g, 1, e + 1, e * 2 + d, e * TT + dt, dp)

            def pair_lo(key, dst_hi, dst_lo):
                w = use[key]
                for i in range(2):
                    att_his[0] += 1
                    dve.wait_ge(att_hi_ready, att_his[0])
                    last = nc.vector.tensor_tensor(dst_lo[:, 2 * key[2] + i, :], work[:, w % 2 * 2 + i, :],
                                                   dst_hi[:, 2 * key[2] + i, :], ALU.subtract)
                last.then_inc(pair_free, 1)

            def maxima(c, i):
                dve.wait_ge(score_ready, TT * c + i + 1)
                n = (i + 1) * P
                link(nc.vector.tensor_tensor(acc[:, i, n - P:n], acc[:, i, n - P:n], causal[:, :], ALU.add))
                link(nc.vector.reduce_max(rowmax[:, i:i + 1], acc[:, i, 0:n], AX.X))
                nc.vector.tensor_scalar(negmax[:, i:i + 1], rowmax[:, i:i + 1], -SCORE_SCALE, None,
                                        ALU.mult).then_inc(max_ready, 1)

            def p_lo(c, i):
                w = use["p", c, i]
                att_his[0] += 1
                dve.wait_ge(att_hi_ready, att_his[0])
                n = (i + 1) * P
                nc.vector.tensor_tensor(hid_lo[i % 2][:, 0:n], work[:, w % 2 * 2, 0:n],
                                        hid_hi[i % 2][:, 0:n], ALU.subtract).then_inc(pair_free, 1)

            def attended(c, i):
                link(nc.vector.reciprocal(rowinv[:, i:i + 1], rowsum[:, i:i + 1]))
                dve.wait_ge(acc_ready, tile_no[1, c] + i + 1)
                nc.vector.scalar_tensor_tensor(x[:, c * TT + i, :], acc[:, i, :], rowinv[:, i:i + 1],
                                               x[:, c * TT + i, :], ALU.mult, ALU.add).then_inc(acc_free, 1)

            def attention(li):
                pair_lo(("q", 0, 0), qT_hi, qT_lo)
                lp, gp = li - 1, len(SIZES[LAYERS[li - 1]]) - 1
                add_tiles(lp, tile_no[lp, gp, CH - 1], CH - 1)
                pair_lo(("q", 0, 1), qT_hi, qT_lo)
                finish_chunk(lp, gp, CH - 1)
                for c in range(CH):
                    more = c + 1 < CH
                    first = ("x", 1, c + 2) if c < 2 else ("x", 2, c - 1)
                    for i in range(TT):
                        maxima(c, i)
                    pair_lo(("v", c, 0), v_hi, v_lo)
                    p_lo(c, 0)
                    pair_lo(("v", c, 1), v_hi, v_lo)
                    transpose_pair(first + (0,))
                    normalise(first + (1,))
                    p_lo(c, 1)
                    if more:
                        pair_lo(("q", c + 1, 0), qT_hi, qT_lo)
                    attended(c, 0)
                    p_lo(c, 2)
                    transpose_pair(first + (1,))
                    if c == 1:
                        normalise(("x", 2, 0, 0))
                    if more:
                        pair_lo(("q", c + 1, 1), qT_hi, qT_lo)
                    else:
                        for part in range(3):
                            split_part(li + 1, 0, part, parts_no[li + 1, 0] - 2 + part)
                    attended(c, 1)
                    p_lo(c, 3)
                    if c == 1:
                        transpose_pair(("x", 2, 0, 0))
                        normalise(("x", 2, 0, 1))
                    attended(c, 2)
                    if c == 1:
                        transpose_pair(("x", 2, 0, 1))
                    attended(c, 3)
                    dve.wait_ge(acc_free, tile_no[li, c] + TT)
                    norm_stats(li + 1, c)
                    if c == 0:
                        normalise(("x", 1, CH - 1, 0))
                    elif c < CH - 1:
                        normalise(("x", 2, c, 0))

            for part in (0, 1):
                split_part(0, 0, part, part + 1)
            for j in (2, 3):
                dve.wait_ge(scratch_done[j], 64)
            normalise(("x", 0, 0, 0))
            mix_split(1)
            transpose_pair(("x", 0, 0, 0))
            normalise(("x", 0, 0, 1))
            transpose_pair(("x", 0, 0, 1))
            normalise(("x", 0, 1, 0))
            split_part(0, 0, 2, 3)
            transpose_pair(("x", 0, 1, 0))
            normalise(("x", 0, 1, 1))
            transpose_pair(("x", 0, 1, 1))
            norm_stats(0, 2, True)
            norm_stats(0, 3, True)
            normalise(("x", 0, 2, 0))
            for li, kind in enumerate(LAYERS):
                G = len(SIZES[kind])
                if kind == "B" and li < LAST:
                    dve.wait_ge(down_s_in, 16)
                    link(nc.vector.tensor_scalar(half_down_s[:, :], half_down_s[:, :], 0.5, None, ALU.mult))
                if kind == "T":
                    attention(li)
                elif kind == "A":
                    group(li, 0)
                    with dve.Fori(0, (G - 2) // 2) as o:
                        group(li, 1, o * 16, o * 32, o * 6)
                        group(li, 2, o * 16, o * 32, o * 6)
                    group(li, G - 1)
                else:
                    for g in range(G):
                        group(li, g)
            add_tiles(LAST, tile_no[LAST, len(SIZES["B"]) - 1, CH - 1], CH - 1)


def _counts():
    raw, n = {}, -32
    for li, kind in enumerate(LAYERS):
        for g in range(len(SIZES[kind])):
            n += 32 if kind == "S" else 48
            raw[li, g] = n
    return raw


raw_count = _counts()


def kernel(**inputs):
    import concourse.bacc as bacc
    from concourse.bass_utils import run_bass_kernel_spmd

    a = {k: np.asarray(v) for k, v in inputs.items()}

    def up_blocks(w):
        h = w.shape[0]
        return w.reshape(h // P, P, KD, P).transpose(0, 3, 2, 1).reshape(h // P, P, KD * P)

    def down_blocks(w):
        return w.T.reshape(w.shape[1] // P, P, D)

    def rows(w):
        return w.reshape(KD, P, w.shape[1]).transpose(1, 0, 2)

    def column(v):
        return v.reshape(-1, P).T

    hadamard = np.array([[1.0]], np.float32)
    while len(hadamard) < P:
        hadamard = np.block([[hadamard, hadamard], [hadamard, -hadamard]])
    causal = np.where(np.arange(P)[None, :] <= np.arange(P)[:, None], 0.0, MASKED).astype(np.float32)
    qkv = a["L0_attn_qkv"]
    arrays = {
        "x": a["L0_attn_x"].reshape(CH * TT, P, D).transpose(1, 0, 2),
        "w1a": up_blocks(a["L0_ffn_W1"]),
        "w3a": up_blocks(a["L0_ffn_W3"]),
        "w2a": a["L0_ffn_W2"].reshape(4, P, HA // P, P).transpose(0, 3, 2, 1),
        "att_w": np.stack([rows(qkv[:, 0:D].T), rows(qkv[:, D:2 * D].T), rows(qkv[:, 2 * D:].T),
                           rows(a["L0_attn_o_proj"])]),
        "gate": up_blocks(a["L1_ffn_gate_w"]),
        "up": up_blocks(a["L1_ffn_up_w"]),
        "down": down_blocks(a["L1_ffn_down_w"]),
        "b": up_blocks(a["L1_attn_B"]),
        "c": down_blocks(a["L1_attn_C"]),
        "small": np.concatenate([column(a["L0_attn_gamma"]), column(a["L0_attn_beta"]),
                                 column(a["L1_ffn_gate_s"]), column(a["L1_ffn_up_s"])], axis=1),
        "down_s": np.broadcast_to(a["L1_ffn_down_s"][None, :], (P, D)),
        "skip_d": np.broadcast_to(a["L1_attn_D"][None, :], (P, D)),
        "ident": np.eye(P, dtype=np.float32),
        "hadamard": hadamard,
        "causal": causal,
    }
    arrays = {k: np.ascontiguousarray(v) for k, v in arrays.items()}
    nc = bacc.Bacc("TRN2", target_bir_lowering=False, num_devices=1)
    t = {k: nc.dram_tensor(f"in_{k}", v.shape, F32, kind="ExternalInput").ap() for k, v in arrays.items()}
    t["out"] = nc.dram_tensor("out_x", (P, CH * TT, D), F32, kind="ExternalOutput").ap()
    build(nc, t)
    r = run_bass_kernel_spmd(nc, [{f"in_{k}": v for k, v in arrays.items()}], core_ids=[0])
    out = r.results[0]["out_x"]
    return np.ascontiguousarray(out.transpose(1, 0, 2).reshape(CH, TOK, D))
```

```python
from contextlib import ExitStack

import numpy as np

import concourse.bass as bass
import concourse.mybir as mybir
from concourse.alu_op_type import AluOpType as ALU

F32 = mybir.dt.float32
F32R = mybir.dt.float32r
I32 = mybir.dt.int32
MAX = bass.bass_isa.ReduceOp.max
ACT = mybir.ActivationFunctionType
AX = mybir.AxisListType

P = 128
D = 512
KD = D // P
CH = 4
TOK = 512
TT = TOK // P
HA = 2048
HB = 1408
HS = 256
EPS = 1e-5
SCORE_SCALE = D ** -0.5
MASKED = -3e38

SIZES = {"A": [2] * (HA // 256), "B": [2, 2, 2, 2, 1, 2], "S": [2], "T": []}
LAYERS = ["A", "T", "A", "B", "S", "B"]
LAST = len(LAYERS) - 1
FIRST_B = LAYERS.index("B")
assert sum(SIZES["A"]) * P == HA and sum(SIZES["B"]) * P == HB and sum(SIZES["S"]) * P == HS


class Plan:

    def __init__(self):
        self.use, self.block, self.tile, self.parts = {}, {}, {}, {}
        self.after = {}
        use = block = tile = parts = 0
        for half in (0, 1):
            self.use["x", 0, 0, half] = use
            use += 1
        for li, kind in enumerate(LAYERS):
            if kind == "T":
                for j in (0, 1):
                    self.use["q", 0, j] = use
                    use += 1
                for c in range(CH):
                    self.tile[li, c] = tile
                    tile += TT
                    for key in attention_uses(c):
                        self.use[key] = use
                        use += 1
                continue
            sizes = SIZES[kind]
            for g, size in enumerate(sizes):
                parts += 2 if kind == "S" else 3
                self.parts[li, g] = parts
                for c in range(CH):
                    self.tile[li, g, c] = tile
                    tile += TT
                    for b in range(size):
                        self.use[li, g, c, b] = use
                        self.block[li, g, c, b] = block
                        use, block = use + 1, block + 1
                        key = None
                        if li == 0 and g == 0 and c < CH - 1:
                            key = ("x", 0, c + 1, b)
                        if li and g == 0 and c in (0, 1) and not (c == 0 and li and LAYERS[li - 1] == "T"):
                            key = ("x", li, c + 2, b)
                        if g == len(sizes) - 1 and c in (2, 3) and li < LAST:
                            key = ("x", li + 1, c - 2, b)
                        if key:
                            self.after[li, g, c, b] = key
                            self.use[key] = use
                            use += 1
        self.tiles = tile


def attention_uses(c):
    first = ("x", 1, c + 2) if c < 2 else ("x", 2, c - 1)
    keys = [("v", c, 0), ("v", c, 1), first + (0,)]
    keys += [("q", c + 1, 0)] if c + 1 < CH else []
    keys += [first + (1,)]
    keys += [("q", c + 1, 1)] if c + 1 < CH else []
    keys += [("x", 2, 0, 0), ("x", 2, 0, 1)] if c == 1 else []
    return keys


def previous(li, g):
    if g:
        return li, g - 1
    if li == 0 or LAYERS[li - 1] == "T":
        return None
    return li - 1, len(SIZES[LAYERS[li - 1]]) - 1


def following(li, g):
    if g + 1 < len(SIZES[LAYERS[li]]):
        return li, g + 1
    if li == LAST or LAYERS[li + 1] == "T":
        return None
    return li + 1, 0


def part_split(li, g, c):
    ln, gn = following(li, g)
    late = g == 0 and previous(li, g) is None
    part = c - 1 if late else c
    if not 0 <= part < 3 or (LAYERS[ln] == "S" and part == 1):
        return None
    return part


def group_buffer(li, g):
    return (sum(len(SIZES[k]) for k in LAYERS[:li]) + g) % 2


def build(nc, t):
    plan = Plan()
    use, block_no, tile_no, parts_no = plan.use, plan.block, plan.tile, plan.parts

    w2_scratch = nc.dram_tensor("w2_scratch", [HA // P, P, D], F32).ap()

    with ExitStack() as ctx:
        def sb(name, shape, dt=F32):
            return ctx.enter_context(nc.sbuf_tensor(name, shape, dt))

        def sem(name):
            return ctx.enter_context(nc.semaphore(name))

        mix_at = -(-nc.sbuf_base // 64) * 64
        mix_hi = sb("mix_hi", [P, 2, KD, D], F32R)
        mix_lo = sb("mix_lo", [P, 2, KD, D], F32R)
        x = sb("x", [P, CH * TT, D])
        xT_hi = sb("xT_hi", [P, CH, KD, TOK], F32R)
        xT_lo_at = -(-nc.sbuf_base // 64) * 64
        xT_lo = sb("xT_lo", [P, CH, KD, TOK], F32R)
        raw = sb("raw", [P, 3, 2 * D])
        w_hi = [sb(f"w_hi{i}", [P, 3, 2 * D], F32R) for i in range(2)]
        w_lo = [sb(f"w_lo{i}", [P, 3, 2 * D], F32R) for i in range(2)]
        hid = [sb(f"hid{i}", [P, TOK]) for i in range(2)]
        hid_hi = [sb(f"hid_hi{i}", [P, TOK], F32R) for i in range(2)]
        hid_lo = [sb(f"hid_lo{i}", [P, TOK], F32R) for i in range(2)]
        xn = [sb(f"xn{i}", [P, D]) for i in range(2)]
        ident = sb("ident", [P, P])
        causal = sb("causal", [P, P])
        half_down_s = sb("half_down_s", [P, D])
        diag_hi = nc.alloc_sbuf_tensor_at("diag_hi", [P, KD, P], F32R, offset=mix_at)
        diag_lo = nc.alloc_sbuf_tensor_at("diag_lo", [P, KD, P], F32R, offset=mix_at + 4 * D)
        diag = nc.alloc_sbuf_tensor_at("diag", [P, KD, P], F32, offset=mix_at + 48 * D)
        waiting = nc.alloc_sbuf_tensor_at("waiting", [P, CH, KD, TOK], F32, offset=xT_lo_at)
        low_abs = nc.alloc_sbuf_tensor_at("low_abs", [P, 2 * D], F32, offset=mix_at + 8 * D)
        scaled = nc.alloc_sbuf_tensor_at("scaled", [P, TT, D], F32, offset=mix_at + 32 * D)
        small = sb("small", [P, 3 * KD + 2 * (HB // P)])
        gamma, beta = small[:, 0:KD], small[:, KD:2 * KD]
        skip_d = small[:, 2 * KD:3 * KD]
        gate_s = small[:, 3 * KD:3 * KD + HB // P]
        up_s = small[:, 3 * KD + HB // P:]
        stats = sb("stats", [P, TT, 6])
        meanvar = sb("meanvar", [P, CH * TT, 2])
        rstd = sb("rstd", [P, CH * TT])
        stats2 = sb("stats2", [P, 2, 6])
        meanvar2 = sb("meanvar2", [P, 2, 2])
        rstd2 = sb("rstd2", [P, 2])
        shift2 = sb("shift2", [P, 2])
        var_eps = sb("var_eps", [P, TT])
        minus_mean2 = var_eps[:, 2:4]
        minus_half = sb("minus_half", [P, TT])
        low_sum = nc.alloc_sbuf_tensor_at("low_sum", [P, len(SIZES["B"]), 4], F32, offset=mix_at + 52 * D)
        inexact = sb("inexact", [P, len(SIZES["B"])], I32)
        rowmax = sb("rowmax", [P, TT])
        negmax = sb("negmax", [P, TT])
        rowsum = sb("rowsum", [P, TT])
        rowinv = sb("rowinv", [P, TT])

        qT_hi = w_hi[0][:, 0:2, :].rearrange("p a (k t) -> p (a k) t", k=2)
        qT_lo = w_lo[0][:, 0:2, :].rearrange("p a (k t) -> p (a k) t", k=2)
        v_hi = w_hi[1][:, 0:2, :].rearrange("p a (k t) -> p (a k) t", k=2)
        v_lo = w_lo[1][:, 0:2, :].rearrange("p a (k t) -> p (a k) t", k=2)

        work = ctx.enter_context(nc.psum_tensor("work", [P, 4, D], F32))
        acc = ctx.enter_context(nc.psum_tensor("acc", [P, 4, D], F32))

        consts_in = sem("consts_in")
        x_in = [sem(f"x_in{c}") for c in range(CH)]
        raw_in = sem("raw_in")
        pair_full = sem("pair_full")
        pair_free = sem("pair_free")
        act_ready = sem("act_ready")
        hid_hi_ready = sem("hid_hi_ready")
        hid_lo_ready = sem("hid_lo_ready")
        acc_ready = sem("acc_ready")
        acc_free = sem("acc_free")
        w_hi_ready = sem("w_hi_ready")
        w_ready = sem("w_ready")
        low_ready = sem("low_ready")
        flag_ready = sem("flag_ready")
        last_added = sem("last_added")
        x_added = sem("x_added")
        xn_ready = sem("xn_ready")
        xT_hi_ready = sem("xT_hi_ready")
        affine_ready = sem("affine_ready")
        stats_ready = sem("stats_ready")
        rstd_ready = sem("rstd_ready")
        stats2_ready = sem("stats2_ready")
        rstd2_ready = sem("rstd2_ready")
        att_hi_ready = sem("att_hi_ready")
        score_ready = sem("score_ready")
        max_ready = sem("max_ready")
        exp_ready = sem("exp_ready")
        table_in = sem("table_in")
        p_full = sem("p_full")
        p_ready = sem("p_ready")
        dve_step = sem("dve_step")
        pool_step = sem("pool_step")
        diag_ready = sem("diag_ready")
        half_ready = sem("half_ready")
        y_added = sem("y_added")
        down_s_in = sem("down_s_in")
        out_done = sem("out_done")
        fw_in = [sem(f"fw_in{i}") for i in range(4)]
        had_in = sem("had_in")
        first_in = sem("first_in")
        had_ready = sem("had_ready")
        fw_hi_ready = sem("fw_hi_ready")
        fw_ready = sem("fw_ready")
        fw_full = sem("fw_full")
        fw_out = sem("fw_out")
        scratch_done = [sem(f"scratch_done{j}") for j in range(4)]
        fly_ready = sem("fly_ready")
        att_w_in = [sem(f"att_w_in{i}") for i in range(4)]
        att_w_hi = sem("att_w_hi")
        att_w_ready = sem("att_w_ready")
        att_vo_ready = sem("att_vo_ready")
        mix_full = sem("mix_full")
        mix_hi_ready = sem("mix_hi_ready")
        mix_ready = sem("mix_ready")

        fw_buf = [x[:, 8:12, :], x[:, 12:16, :]]
        fw_tmp = x[:, 4:8, :]
        fw_parts = [(xT_hi[:, 3, :, :], xT_lo[:, 3, :, :]), (v_hi, v_lo)]
        stage = [hid[0], hid[1], xn[0], xn[1]]
        had_raw = half_down_s[:, 0:P]
        had = hid_hi[0][:, 0:P]
        neg_had = hid_hi[0][:, P:2 * P]
        att_raw = [nc.alloc_sbuf_tensor_at(f"att_raw{i}", [P, KD, D], F32, offset=mix_at + 16 * D * at)[:, :, :]
                   for i, at in enumerate((0, 2, 1, 3))]
        att_at = [1, 2, 1, 2]

        def added_no(li, tile):
            before = TT * CH * len(SIZES["B"]) if li == LAST else 0
            return tile - tile_no[li, 0, 0] + before

        def normed_tile(c, half, j):
            return waiting[:, c, 2 * j:2 * j + 2, half * 2 * P:(half + 1) * 2 * P]

        def halves(tile):
            return tile.rearrange("p (a n) -> p a n", a=2)

        block = ctx.enter_context(nc.Block())

        def three(pe, out, a_hi, a_lo, b_hi, b_lo, start, stop, zero=None):
            pe.matmul(out, a_hi, b_hi, start=start, stop=False)
            if zero != "b":
                last = pe.matmul(out, a_hi, b_lo, start=False, stop=stop and zero == "a")
            if zero != "a":
                last = pe.matmul(out, a_lo, b_hi, start=False, stop=stop)
            return last

        @block.sync
        def _(sp):
            sp.dma_start(had_raw, t["hadamard"]).then_inc(had_in, 16)
            for i in (0, 1):
                sp.dma_start(att_raw[i], t["att_w"][i]).then_inc(att_w_in[i], 16)

            def slice_in(s):
                sp.dma_start(fw_buf[s % 2].rearrange("p a (b d) -> p (a b) d", b=4),
                             t["w2a"][s]).then_inc(fw_in[s], 16)

            slice_in(0)
            slice_in(1)
            sp.dma_start(ident[:, :], t["ident"]).then_inc(consts_in, 16)
            sp.dma_start(causal[:, :], t["causal"]).then_inc(consts_in, 16)
            sp.dma_start(small[:, :], t["small"]).then_inc(consts_in, 16)
            sp.dma_start(x[:, 0:TT, :], t["x"][:, 0:TT, :]).then_inc(x_in[0], 16)
            sp.wait_ge(fw_ready, 1)
            slice_in(2)
            for i in (2, 3):
                sp.dma_start(att_raw[i], t["att_w"][i]).then_inc(att_w_in[i], 16)
            sp.wait_ge(fw_ready, 2)
            slice_in(3)
            for part, name in ((0, "w1a"), (1, "w3a")):
                sp.dma_start(raw[:, part, :].rearrange("p (b n) -> p b n", b=2),
                             t[name][0:2, :, :].rearrange("b p n -> p b n")).then_inc(first_in, 16)
            sp.wait_ge(fly_ready, 4)
            sp.dma_start(x[:, TT:2 * TT, :], t["x"][:, TT:2 * TT, :]).then_inc(x_in[1], 16)
            for c in (2, 3):
                sp.wait_ge(fw_ready, c + 1)
                sp.dma_start(x[:, c * TT:(c + 1) * TT, :], t["x"][:, c * TT:(c + 1) * TT, :]
                             ).then_inc(x_in[c], 16)

            def load(src, b0, size, parts=(0, 1, 2)):
                for part in parts:
                    sp.dma_start(
                        raw[:, part, 0:size * D].rearrange("p (b n) -> p b n", b=size),
                        src[part][bass.ds(b0, size), :, :].rearrange("b p n -> p b n")
                    ).then_inc(raw_in, 16)

            sources = {"A": (t["w1a"], t["w3a"], w2_scratch), "B": (t["gate"], t["up"], t["down"]),
                       "S": (t["b"], None, t["c"])}
            for j in range(4):
                sp.wait_ge(scratch_done[j], 64)
            for li, kind in enumerate(LAYERS):
                b0 = 0
                if kind == "B" and li < LAST:
                    sp.wait_ge(acc_free, tile_no[1, CH - 1] + TT)
                    sp.dma_start(half_down_s[:, :], t["down_s"]).then_inc(down_s_in, 16)
                for g, size in enumerate(SIZES[kind]):
                    if kind == "A" and g:
                        break
                    if li or g:
                        before = previous(li, g) or (0, len(SIZES["A"]) - 1)
                        sp.wait_ge(w_ready, parts_no[before])
                        load(sources[kind], b0, size, (0, 2) if kind == "S" else (0, 1, 2))
                    else:
                        load(sources[kind], b0, size, (2,))
                    b0 += size
                if kind == "A":
                    with sp.Fori(1, len(SIZES["A"])) as g:
                        sp.wait_ge(w_ready, (parts_no[li, 0] - 3) + g * 3)
                        load(sources[kind], g * 2, 2)
            for c in range(CH - 1):
                sp.wait_ge(x_added, added_no(LAST, tile_no[LAST, len(SIZES["B"]) - 1, c]) + TT)
                sp.dma_start(t["out"][:, c * TT:(c + 1) * TT, :],
                             x[:, c * TT:(c + 1) * TT, :]).then_inc(out_done, 16)
            for i in range(TT):
                if i % 2:
                    sp.wait_ge(last_added, i // 2 + 1)
                else:
                    sp.wait_ge(x_added, added_no(LAST, plan.tiles) - TT + i // 2 + 1)
                at = (CH - 1) * TT + i
                sp.dma_start(t["out"][:, at, :], x[:, at, :]).then_inc(out_done, 16)
            sp.wait_ge(out_done, 16 * (CH - 1 + TT))

        @block.tensor
        def _(pe):
            def mix(m, ready, n):
                pe.wait_ge(ready, n)
                a, b = att_at[2 * m], att_at[2 * m + 1]
                for k in range(KD):
                    if m:
                        pe.wait_ge(fw_out, 8 + k + 1)
                    for j in range(KD):
                        last = three(pe, (acc if m else work)[:, k, :],
                                     xT_hi[:, a, j, k * P:(k + 1) * P], xT_lo[:, a, j, k * P:(k + 1) * P],
                                     xT_hi[:, b, j, :], xT_lo[:, b, j, :], j == 0, j == KD - 1)
                    last.then_inc(mix_full, 1)

            mix(0, att_w_ready, 2)
            pe.wait_ge(had_ready, 2)
            for s in range(4):
                pe.wait_ge(fw_ready, s + 1)
                hi, lo = fw_parts[s % 2]
                banks = work if s % 2 else acc
                for j in range(4):
                    if s == 1:
                        pe.wait_ge(mix_ready, j + 1)
                    if s >= 2:
                        pe.wait_ge(fw_out, 4 * (s - 2) + j + 1)
                    for i in range(4):
                        sign = neg_had if bin(i & j).count("1") % 2 else had
                        pe.matmul(banks[:, j, :], sign, hi[:, i, :], start=i == 0, stop=False)
                        last = pe.matmul(banks[:, j, :], sign, lo[:, i, :], start=False, stop=i == 3)
                    last.then_inc(fw_full, 1)
            mix(1, att_vo_ready, 2)
            pe.wait_ge(fw_out, 16)

            xn_pairs = [0]

            def pair_wait(w):
                if isinstance(w, int) and w < 2:
                    return
                pe.wait_ge(pair_free, w - 1)

            def transpose_pair(key):
                w = use[key]
                pair_wait(w)
                xn_pairs[0] += 1
                pe.wait_ge(xn_ready, 2 * xn_pairs[0])
                for j in range(2):
                    tile = normed_tile(key[2], key[3], j)
                    for k in range(KD):
                        last = pe.transpose(work[:, w % 2 * 2 + j, k * P:(k + 1) * P],
                                            tile[:, k // 2, k % 2 * P:(k % 2 + 1) * P], ident[:, :])
                last.then_inc(pair_full, 1)

            def up(w, pair, c, buf, b, matrices, exact=False):
                pair_wait(w)
                for m in range(matrices):
                    for k in range(KD):
                        at = slice(b * D + k * P, b * D + (k + 1) * P)
                        last = three(pe, work[:, 2 * pair + m, :], w_hi[buf][:, m, at], w_lo[buf][:, m, at],
                                     xT_hi[:, c, k, :], xT_lo[:, c, k, :], k == 0, k == KD - 1,
                                     "a" if exact else None)
                last.then_inc(pair_full, 1)

            def down(n, h, buf, b, size, tile, exact=False, skip=None):
                pe.wait_ge(hid_lo_ready, n + 1)
                at = slice(b * D, (b + 1) * D)
                for i in range(TT):
                    if b == 0 and not (isinstance(tile, int) and tile < TT):
                        pe.wait_ge(acc_free, tile - 3 + i)
                    ts = slice(i * P, (i + 1) * P)
                    last = three(pe, acc[:, i, :], hid_hi[h][:, ts], hid_lo[h][:, ts],
                                 w_hi[buf][:, 2, at], w_lo[buf][:, 2, at], b == 0, b == size - 1,
                                 "b" if exact else None)
                    if skip is not None:
                        for k in range(KD):
                            last = three(pe, acc[:, i, k * P:(k + 1) * P], xT_hi[:, skip, k, ts],
                                         xT_lo[:, skip, k, ts], diag_hi[:, k, :], diag_lo[:, k, :],
                                         False, False)
                    if b == size - 1:
                        last.then_inc(acc_ready, 1)

            def both_ways(flag, emit):
                at = xn_pairs[0]
                with pe.If(flag == 0):
                    emit(True)
                xn_pairs[0] = at
                with pe.Else():
                    emit(False)

            flags = {}

            def down_before(li, g, c0, d, dt, exact):
                n = block_no[li, g, c0, 0] - 1
                tile = tile_no[li, g, c0] - TT + dt
                if c0:
                    size = SIZES[LAYERS[li]][g]
                    down(n + d, n % 2, group_buffer(li, g), size - 1, size, tile, exact)
                elif previous(li, g):
                    lp, gp = previous(li, g)
                    size = SIZES[LAYERS[lp]][gp]
                    emit = lambda e: down(n + d, n % 2, group_buffer(lp, gp), size - 1, size, tile, e)
                    if (lp, gp) in flags:
                        both_ways(flags[lp, gp], emit)
                    else:
                        emit(False)

            def up_block(li, g, c0, c, b, d, exact):
                w = use[li, g, c0, b]
                up(w + d, w % 2, c, group_buffer(li, g), b, 1 if LAYERS[li] == "S" else 2, exact)

            def rest(li, g, c0, c, d, dt, exact):
                size, buf = SIZES[LAYERS[li]][g], group_buffer(li, g)
                for b in range(size):
                    if b:
                        up_block(li, g, c0, c, b, d, exact)
                    key = plan.after.get((li, g, c0, b))
                    late = b and key and (LAYERS[key[1]] == "T" or LAYERS[li] != "A")
                    if key and not late:
                        transpose_pair(key)
                    if b:
                        n = block_no[li, g, c0, b] - 1
                        if LAYERS[li] == "S" and c0 == 0:
                            pe.wait_ge(diag_ready, 2 * KD + 1)
                        down(n + d, n % 2, buf, b - 1, size, tile_no[li, g, c0] + dt, exact,
                             c0 if LAYERS[li] == "S" else None)
                    if late:
                        transpose_pair(key)

            def other_steps(li, g, d, dt, exact):
                if g in (0, len(SIZES[LAYERS[li]]) - 1) or SIZES[LAYERS[li]][g] == 1:
                    for c in range(1, CH):
                        if g == 0:
                            pe.wait_ge(pair_free, use["x", li, c, 1] + 1)
                        up_block(li, g, c, c, 0, d, exact)
                        down_before(li, g, c, d, dt, exact)
                        rest(li, g, c, c, d, dt, exact)
                else:
                    with pe.Fori(0, CH - 1) as e:
                        de, dte = e * 2 + d, e * TT + dt
                        up_block(li, g, 1, e + 1, 0, de, exact)
                        down_before(li, g, 1, de, dte, exact)
                        rest(li, g, 1, e + 1, de, dte, exact)

            def group(li, g, d=0, dt=0, dp=0):
                first = (li, g) == (0, 0)
                pe.wait_ge(w_ready, 2 if first else parts_no[li, g] + dp)
                if g == 0:
                    pe.wait_ge(pair_free, use["x", li, 0, 1] + 1)
                if LAYERS[li] != "B":
                    up_block(li, g, 0, 0, 0, d, False)
                    down_before(li, g, 0, d, dt, False)
                    if first:
                        pe.wait_ge(w_ready, 3)
                    rest(li, g, 0, 0, d, dt, False)
                    other_steps(li, g, d, dt, False)
                    return
                pe.wait_ge(flag_ready, g + 1)
                flag = flags[li, g] = pe.value_load(inexact[0:1, g:g + 1], min_val=0, max_val=1)
                both_ways(flag, lambda exact: up_block(li, g, 0, 0, 0, d, exact))
                down_before(li, g, 0, d, dt, False)

                def remaining(exact):
                    rest(li, g, 0, 0, d, dt, exact)
                    other_steps(li, g, d, dt, exact)

                both_ways(flag, remaining)

            def q_pair(c, j):
                w = use["q", c, j]
                pair_wait(w)
                for i in range(2):
                    m = slice((2 * j + i) * P, (2 * j + i + 1) * P)
                    for k in range(KD):
                        last = three(pe, work[:, w % 2 * 2 + i, :], mix_hi[:, 0, k, m], mix_lo[:, 0, k, m],
                                     xT_hi[:, c, k, :], xT_lo[:, c, k, :], k == 0, k == KD - 1)
                last.then_inc(pair_full, 1)

            def v_pair(c, j):
                w = use["v", c, j]
                pair_wait(w)
                for i in range(2):
                    m = slice((2 * j + i) * P, (2 * j + i + 1) * P)
                    for k in range(KD):
                        last = three(pe, work[:, w % 2 * 2 + i, :], xT_hi[:, c, k, m], xT_lo[:, c, k, m],
                                     mix_hi[:, 1, k, :], mix_lo[:, 1, k, :], k == 0, k == KD - 1)
                last.then_inc(pair_full, 1)

            def scores(c, i):
                pe.wait_ge(acc_free, tile_no[1, c] - 3 + i)
                n = (i + 1) * P
                for k in range(KD):
                    last = three(pe, acc[:, i, 0:n], qT_hi[:, k, i * P:n], qT_lo[:, k, i * P:n],
                                 xT_hi[:, c, k, 0:n], xT_lo[:, c, k, 0:n], k == 0, k == KD - 1)
                last.then_inc(score_ready, 1)

            def p_transpose(c, i):
                pe.wait_ge(exp_ready, TT * c + i + 1)
                for k in range(i + 1):
                    last = pe.transpose(acc[:, i, k * P:(k + 1) * P],
                                        hid[i % 2][:, k * P:(k + 1) * P], ident[:, :])
                last.then_inc(p_full, 1)

            def attend(c, i):
                if i % 2 == 0:
                    pe.wait_ge(pair_free, use["v", c, i // 2] + 1)
                pe.wait_ge(p_ready, TT * c + i + 1)
                for k in range(i + 1):
                    ks = slice(k * P, (k + 1) * P)
                    last = three(pe, acc[:, i, :], hid_hi[i % 2][:, ks], hid_lo[i % 2][:, ks],
                                 v_hi[:, k, :], v_lo[:, k, :], k == 0, k == i)
                last.then_inc(acc_ready, 1)

            def attention(li):
                pe.wait_ge(pair_free, use["x", li, 0, 1] + 1)
                q_pair(0, 0)
                lp, gp = li - 1, len(SIZES[LAYERS[li - 1]]) - 1
                n = block_no[lp, gp, CH - 1, 1]
                down(n, n % 2, group_buffer(lp, gp), 1, 2, tile_no[lp, gp, CH - 1])
                q_pair(0, 1)
                for c in range(CH):
                    more = c + 1 < CH
                    first = ("x", 1, c + 2) if c < 2 else ("x", 2, c - 1)
                    v_pair(c, 0)
                    pe.wait_ge(pair_free, use["q", c, 1] + 1)
                    for i in range(TT):
                        scores(c, i)
                    p_transpose(c, 0)
                    p_transpose(c, 1)
                    v_pair(c, 1)
                    attend(c, 0)
                    attend(c, 1)
                    p_transpose(c, 2)
                    transpose_pair(first + (0,))
                    if more:
                        pe.wait_ge(pair_free, use["x", li, c + 1, 1] + 1)
                        q_pair(c + 1, 0)
                    p_transpose(c, 3)
                    transpose_pair(first + (1,))
                    attend(c, 2)
                    if more:
                        q_pair(c + 1, 1)
                    if c == 1:
                        transpose_pair(("x", 2, 0, 0))
                    attend(c, 3)
                    if c == 1:
                        transpose_pair(("x", 2, 0, 1))

            pe.wait_ge(consts_in, 48)
            for half in (0, 1):
                transpose_pair(("x", 0, 0, half))
            pe.wait_ge(mix_ready, 2 * KD)
            for li, kind in enumerate(LAYERS):
                G = len(SIZES[kind])
                if kind == "T":
                    attention(li)
                elif kind == "A":
                    group(li, 0)
                    with pe.Fori(0, (G - 2) // 2) as o:
                        group(li, 1, o * 16, o * 32, o * 6)
                        group(li, 2, o * 16, o * 32, o * 6)
                    group(li, G - 1)
                else:
                    for g in range(G):
                        group(li, g)
            g = len(SIZES["B"]) - 1
            n = block_no[LAST, g, CH - 1, 1]
            both_ways(flags[LAST, g], lambda exact: down(n, n % 2, group_buffer(LAST, g), 1, 2,
                                                         tile_no[LAST, g, CH - 1], exact))

        @block.scalar
        def _(act):
            act.wait_ge(had_in, 16)
            nc.scalar.activation(had, had_raw, ACT.Copy).then_inc(had_ready, 1)
            nc.scalar.activation(neg_had, had_raw, ACT.Copy, scale=-1.0).then_inc(had_ready, 1)

            def fw_split(s):
                act.wait_ge(fly_ready, s + 1)
                nc.scalar.activation(fw_parts[s % 2][0], fw_buf[s % 2], ACT.Copy).then_inc(fw_hi_ready, 1)

            def fw_scale(s):
                for j in range(4):
                    act.wait_ge(fw_full, 4 * s + j + 1)
                    if s:
                        act.wait_ge(scratch_done[j], 16 * s)
                    nc.scalar.activation(stage[j][:, :], (work if s % 2 else acc)[:, j, :], ACT.Copy,
                                         scale=0.5 * HA ** -0.5).then_inc(fw_out, 1)
                    act.wait_ge(fw_out, 4 * s + j + 1)
                    act.dma_start(
                        w2_scratch[4 * j:4 * j + 4, :, s * P:(s + 1) * P].rearrange("b p d -> p b d"),
                        stage[j][:, :].rearrange("p (b d) -> p b d", b=4)).then_inc(scratch_done[j], 16)

            def att_split(i):
                act.wait_ge(att_w_in[i], 16)
                nc.scalar.activation(xT_hi[:, att_at[i], :, :], att_raw[i], ACT.Copy).then_inc(att_w_hi, 1)

            def mix_split(m):
                for k in range(KD):
                    act.wait_ge(mix_full, KD * m + k + 1)
                    nc.scalar.activation(mix_hi[:, m, k, :], (acc if m else work)[:, k, :],
                                         ACT.Copy).then_inc(mix_hi_ready, 1)

            att_split(0)
            att_split(1)
            fw_split(0)
            fw_split(1)
            act.wait_ge(att_w_ready, 2)
            mix_split(0)
            fw_scale(0)
            fw_split(2)
            att_split(2)
            att_split(3)
            fw_scale(1)
            fw_split(3)
            fw_scale(2)
            act.wait_ge(first_in, 32)
            for part in (0, 1):
                nc.scalar.activation(w_hi[0][:, part, :], raw[:, part, :], ACT.Copy).then_inc(w_hi_ready, 1)
            fw_scale(3)
            act.wait_ge(att_vo_ready, 2)
            mix_split(1)

            affine_pairs = [0]

            def split_part(li, g, part):
                size, buf = SIZES[LAYERS[li]][g], group_buffer(li, g)
                nc.scalar.activation(w_hi[buf][:, part, 0:size * D], raw[:, part, 0:size * D],
                                     ACT.Copy).then_inc(w_hi_ready, 1)

            low_parts = [0]

            def sum_low(g, part, no):
                act.wait_ge(w_ready, no)
                if low_parts[0]:
                    act.wait_ge(low_ready, low_parts[0])
                low_parts[0] += 1
                n = SIZES["B"][g] * D
                nc.scalar.activation(low_abs[:, 0:n], w_lo[group_buffer(FIRST_B, g)][:, part, 0:n].bitcast(F32),
                                     ACT.Abs, accum_out=low_sum[:, g, part:part + 1]).then_inc(low_ready, 1)

            def weights_here(li, g, dr=0):
                act.wait_ge(raw_in, raw_count[li, g] + dr)

            def up(w, pair, n, h, li, blk):
                act.wait_ge(pair_full, w + 1)
                if LAYERS[li] == "S":
                    nc.scalar.activation(hid[h][:, :], work[:, 2 * pair, :], ACT.Tanh).then_inc(act_ready, 1)
                    act.wait_ge(act_ready, n + 1)
                    nc.scalar.activation(hid_hi[h][:, :], hid[h][:, :], ACT.Copy).then_inc(hid_hi_ready, 1)
                    return
                scale = gate_s[:, blk:blk + 1] if LAYERS[li] == "B" else 1.0
                nc.scalar.activation(hid[h][:, :], work[:, 2 * pair, :], ACT.Silu,
                                     scale=scale).then_inc(act_ready, 1)
                act.wait_ge(pair_free, w + 1)
                nc.scalar.activation(hid_hi[h][:, :], hid[h][:, :], ACT.Copy).then_inc(hid_hi_ready, 1)

            def transpose_pair(key):
                w = use[key]
                act.wait_ge(pair_full, w + 1)
                if LAYERS[key[1]] == "T":
                    for k in range(KD):
                        bank = work[:, w % 2 * 2:w % 2 * 2 + 2, k * P:(k + 1) * P]
                        last = nc.scalar.activation(bank, bank, ACT.Identity, bias=beta[:, k:k + 1],
                                                    scale=gamma[:, k:k + 1])
                    last.then_inc(affine_ready, 1)
                    affine_pairs[0] += 1
                    act.wait_ge(affine_ready, affine_pairs[0])
                for j in range(2):
                    ts = slice((2 * key[3] + j) * P, (2 * key[3] + j + 1) * P)
                    nc.scalar.activation(
                        xT_hi[:, key[2], :, ts],
                        work[:, w % 2 * 2 + j, :].rearrange("p (k t) -> p k t", k=KD),
                        ACT.Copy).then_inc(xT_hi_ready, 1)

            second_pairs = [0]

            def normalise2(c, half):
                second_pairs[0] += 1
                act.wait_ge(rstd2_ready, second_pairs[0])
                for j in range(2):
                    nc.scalar.activation(normed_tile(c, half, j), halves(xn[j][:, :]), ACT.Identity,
                                         bias=shift2[:, j:j + 1], scale=rstd2[:, j:j + 1]).then_inc(xn_ready, 1)

            def step(li, g, c0, c, d=0, dr=0):
                second = isinstance(c, int) and LAYERS[min(li + 1, LAST)] == "T" and g == len(SIZES[LAYERS[li]]) - 1
                for b in range(SIZES[LAYERS[li]][g]):
                    w, n = use[li, g, c0, b], block_no[li, g, c0, b]
                    up(w + d, w % 2, n + d, n % 2, li, sum(SIZES[LAYERS[li]][:g]) + b)
                    if b == 0 and following(li, g) and part_split(li, g, c0) is not None:
                        ln, gn = following(li, g)
                        weights_here(ln, gn, dr)
                        split_part(ln, gn, c if part_split(li, g, c0) == c0 else c - 1)
                    if second and b and c > 1:
                        normalise2(c - 2, 1)
                    if (li, g, c0, b) in plan.after:
                        transpose_pair(plan.after[li, g, c0, b])
                if second and c:
                    normalise2(c - 1, 0)
                if following(li, g) and following(li, g)[0] == FIRST_B and part_split(li, g, c0) is not None:
                    ln, gn = following(li, g)
                    sum_low(gn, c, parts_no[ln, gn] - 2 + c)

            def group(li, g, d=0, dr=0):
                step(li, g, 0, 0, d, dr)
                G = len(SIZES[LAYERS[li]])
                if g in (0, G - 1) or LAYERS[li] == "B":
                    for c in range(1, CH):
                        step(li, g, c, c, d, dr)
                else:
                    with act.Fori(0, CH - 2) as e:
                        step(li, g, 1, e + 1, e * 2 + d, dr)
                    step(li, g, CH - 1, CH - 1, d, dr)

            def pair_hi(key, dst):
                w = use[key]
                act.wait_ge(pair_full, w + 1)
                for i in range(2):
                    nc.scalar.activation(dst[:, 2 * key[2] + i, :], work[:, w % 2 * 2 + i, :],
                                         ACT.Copy).then_inc(att_hi_ready, 1)

            def numerators(c, i):
                act.wait_ge(max_ready, TT * c + i + 1)
                if i >= 2:
                    act.wait_ge(p_full, TT * c + i - 1)
                n = (i + 1) * P
                nc.scalar.activation(hid[i % 2][:, 0:n], acc[:, i, 0:n], ACT.Exp,
                                     bias=negmax[:, i:i + 1], scale=SCORE_SCALE,
                                     accum_out=rowsum[:, i:i + 1]).then_inc(exp_ready, 1)

            def p_hi(c, i):
                act.wait_ge(p_full, TT * c + i + 1)
                if i >= 2:
                    act.wait_ge(acc_ready, tile_no[1, c] + i - 1)
                n = (i + 1) * P
                nc.scalar.activation(hid_hi[i % 2][:, 0:n], acc[:, i, 0:n],
                                     ACT.Copy).then_inc(att_hi_ready, 1)

            def attention(li):
                for j in range(2):
                    pair_hi(("q", 0, j), qT_hi)
                normalise2(2, 1)
                for c in range(CH):
                    more = c + 1 < CH
                    first = ("x", 1, c + 2) if c < 2 else ("x", 2, c - 1)
                    pair_hi(("v", c, 0), v_hi)
                    numerators(c, 0)
                    numerators(c, 1)
                    if c == 1:
                        normalise2(3, 0)
                    p_hi(c, 0)
                    p_hi(c, 1)
                    numerators(c, 2)
                    numerators(c, 3)
                    pair_hi(("v", c, 1), v_hi)
                    if c == 1:
                        normalise2(3, 1)
                    p_hi(c, 2)
                    transpose_pair(first + (0,))
                    if more:
                        pair_hi(("q", c + 1, 0), qT_hi)
                    p_hi(c, 3)
                    transpose_pair(first + (1,))
                    if more:
                        pair_hi(("q", c + 1, 1), qT_hi)
                    else:
                        weights_here(li + 1, 0)
                        for part in range(3):
                            split_part(li + 1, 0, part)
                    if c == 1:
                        transpose_pair(("x", 2, 0, 0))
                        transpose_pair(("x", 2, 0, 1))

            act.wait_ge(consts_in, 48)
            for half in (0, 1):
                transpose_pair(("x", 0, 0, half))
            weights_here(0, 0)
            split_part(0, 0, 2)
            for j in (0, 1):
                act.wait_ge(scratch_done[j], 64)
            nc.scalar.activation(hid[0][:, 0:1], ident[:, 0:1], ACT.Silu).then_inc(table_in, 1)
            act.wait_ge(table_in, 1)
            for li, kind in enumerate(LAYERS):
                G = len(SIZES[kind])
                if kind == "T":
                    attention(li)
                elif kind == "A":
                    group(li, 0)
                    with act.Fori(0, (G - 2) // 2) as o:
                        group(li, 1, o * 16, o * 96)
                        group(li, 2, o * 16, o * 96)
                    group(li, G - 1)
                else:
                    for g in range(G):
                        group(li, g)

        @block.gpsimd
        def _(pool):
            pool.memset(minus_half[:, :], -0.5).then_inc(pool_step, 1)
            steps = [1]

            def deviation(out, var, n):
                pool.tensor_scalar(var_eps[:, 0:n], var, 1.0, EPS, ALU.mult, ALU.add).then_inc(pool_step, 1)
                steps[0] += 1
                pool.wait_ge(pool_step, steps[0])
                return pool.tensor_tensor(out, var_eps[:, 0:n], minus_half[:, 0:n], ALU.pow)

            done, done2 = [0], [0]

            def var_eps_read():
                if done[0]:
                    pool.wait_ge(rstd_ready, done[0])
                if done2[0]:
                    pool.wait_ge(rstd2_ready, done2[0])

            def chunk(c):
                var_eps_read()
                done[0] += 1
                pool.wait_ge(stats_ready, done[0])
                deviation(rstd[:, c * TT:(c + 1) * TT], meanvar[:, c * TT:(c + 1) * TT, 1], TT
                          ).then_inc(rstd_ready, 1)

            def second():
                var_eps_read()
                done2[0] += 1
                pool.wait_ge(stats2_ready, done2[0])
                pool.tensor_scalar(minus_mean2, meanvar2[:, :, 0], -1.0, 0.0, ALU.mult,
                                   ALU.add).then_inc(pool_step, 1)
                steps[0] += 1
                deviation(rstd2[:, :], meanvar2[:, :, 1], 2).then_inc(pool_step, 1)
                steps[0] += 1
                pool.wait_ge(pool_step, steps[0])
                pool.tensor_tensor(shift2[:, :], minus_mean2, rstd2[:, :],
                                   ALU.mult).then_inc(rstd2_ready, 1)
                for j in range(2):
                    i = 2 * (done2[0] - 1) + j
                    pool.tensor_tensor(x[:, i, :], x[:, i, :], xn[j][:, :], ALU.add).then_inc(y_added, 1)

            def constants_b():
                pool.wait_ge(acc_free, tile_no[1, CH - 1] + TT)
                for k in range(KD):
                    for part in (diag, diag_hi):
                        pool.tensor_scalar(part[:, k, :], ident[:, :], skip_d[:, k:k + 1], 0.0,
                                           ALU.mult, ALU.add).then_inc(diag_ready, 1)
                pool.wait_ge(diag_ready, 2 * KD)
                pool.tensor_tensor(diag_lo[:, :, :], diag[:, :, :], diag_hi[:, :, :],
                                   ALU.subtract).then_inc(diag_ready, 1)
                pool.wait_ge(down_s_in, 16)
                pool.tensor_scalar(half_down_s[:, :], half_down_s[:, :], 0.5, 0.0, ALU.mult,
                                   ALU.add).then_inc(half_ready, 1)

            def flag(g):
                pool.wait_ge(low_ready, 3 * g + 3)
                pool.tensor_tensor(low_sum[:, g, 3:4], low_sum[:, g, 0:1], low_sum[:, g, 1:2],
                                   ALU.add).then_inc(pool_step, 1)
                pool.wait_ge(pool_step, steps[0] + 1)
                pool.tensor_tensor(low_sum[:, g, 0:1], low_sum[:, g, 3:4], low_sum[:, g, 2:3],
                                   ALU.add).then_inc(pool_step, 1)
                pool.wait_ge(pool_step, steps[0] + 2)
                pool.tensor_scalar(low_sum[:, g, 1:2], low_sum[:, g, 0:1], 0.0, 0.0, ALU.is_equal,
                                   ALU.is_equal).then_inc(pool_step, 1)
                pool.wait_ge(pool_step, steps[0] + 3)
                steps[0] += 3
                pool.partition_all_reduce(inexact[:, g:g + 1], low_sum[:, g, 1:2], P, MAX
                                          ).then_inc(flag_ready, 1)

            def add_tiles(tile, c, tiles=range(TT)):
                for i in tiles:
                    pool.wait_ge(acc_free, tile + i + 1)
                    pool.tensor_tensor(x[:, c * TT + i, :], x[:, c * TT + i, :], scaled[:, i, :],
                                       ALU.add).then_inc(x_added, 1)

            def ffn_b(li):
                G = len(SIZES["B"])
                for g in range(G):
                    if g:
                        add_tiles(tile_no[li, g - 1, CH - 1], CH - 1)
                    if g == G - 1:
                        for c in range(CH - 1):
                            add_tiles(tile_no[li, g, c], c)
                            if li < LAST:
                                chunk(c)
                    else:
                        for c in range(CH - 1):
                            before = 1 if SIZES["B"][g] == 1 else 0
                            at = c == CH - 2 - before and li < LAST
                            add_tiles(tile_no[li, g, c], c, range(before))
                            if at:
                                flag(g + 1)
                            add_tiles(tile_no[li, g, c], c, range(before, TT))
                if li < LAST:
                    add_tiles(tile_no[li, G - 1, CH - 1], CH - 1)
                    chunk(CH - 1)
                    return
                for i in (0, 2):
                    pool.wait_ge(acc_free, plan.tiles - TT + i // 2 + 1)
                    at = (CH - 1) * TT + i
                    pool.tensor_tensor(x[:, at, :], x[:, at, :], scaled[:, i, :],
                                       ALU.add).then_inc(x_added, 1)

            for i in (2, 3):
                pool.wait_ge(att_w_hi, i + 1)
                pool.tensor_tensor(xT_lo[:, att_at[i], :, :], att_raw[i], xT_hi[:, att_at[i], :, :],
                                   ALU.subtract).then_inc(att_vo_ready, 1)
            for c in range(CH):
                chunk(c)
            for li in range(1, LAST + 1):
                if LAYERS[li - 1] == "B":
                    ffn_b(li - 1)
                    continue
                if LAYERS[li] == "B" and li < LAST:
                    constants_b()
                if LAYERS[li] != "T":
                    for c in range(CH if LAYERS[li - 1] != "T" else 1):
                        if LAYERS[li] == "B" and li < LAST and c == CH - 2:
                            flag(0)
                        chunk(c)
                    if LAYERS[li - 1] == "T":
                        second()
                        second()
                        for c in range(1, CH):
                            chunk(c)
                else:
                    for c in range(CH):
                        chunk(c)
                        second()
                        if c < CH - 2:
                            second()
            ffn_b(LAST)

        @block.vector
        def _(dve):
            steps = [0]

            def link(ins):
                steps[0] += 1
                ins.then_inc(dve_step, 1)
                dve.wait_ge(dve_step, steps[0])

            chunks = [0]

            def norm_stats(li, c, first=False):
                if chunks[0]:
                    dve.wait_ge(stats_ready, chunks[0])
                chunks[0] += 1
                if first:
                    dve.wait_ge(x_in[c], 16)
                for i in range(TT):
                    last = nc.vector.bn_stats(stats[:, i, :], x[:, c * TT + i, :])
                link(last)
                for i in range(TT):
                    last = nc.vector.bn_aggr(meanvar[:, c * TT + i, :], stats[:, i, :])
                last.then_inc(stats_ready, 1)

            def fly(dst, src, pattern):
                s = src.rearrange("p a (b d) -> p a b d", b=4)
                o = dst.rearrange("p a (b d) -> p a b d", b=4)
                if pattern == 0:
                    lo_s, hi_s, lo_o, hi_o = s[:, :, 0:4:2, :], s[:, :, 1:4:2, :], o[:, :, 0:4:2, :], o[:, :, 1:4:2, :]
                else:
                    lo_s, hi_s, lo_o, hi_o = s[:, :, 0:2, :], s[:, :, 2:4, :], o[:, :, 0:2, :], o[:, :, 2:4, :]
                nc.vector.tensor_tensor(lo_o, lo_s, hi_s, ALU.add)
                return nc.vector.tensor_tensor(hi_o, lo_s, hi_s, ALU.subtract)

            def fw_slice(s):
                buf = fw_buf[s % 2]
                dve.wait_ge(fw_in[s], 16)
                if s:
                    dve.wait_ge(fly_ready, s)
                link(fly(fw_tmp, buf, 0))
                fly(buf, fw_tmp, 1).then_inc(fly_ready, 1)
                dve.wait_ge(fw_hi_ready, s + 1)
                nc.vector.tensor_tensor(fw_parts[s % 2][1], buf, fw_parts[s % 2][0],
                                        ALU.subtract).then_inc(fw_ready, 1)

            def mix_split(m):
                for k in range(KD):
                    dve.wait_ge(mix_hi_ready, KD * m + k + 1)
                    nc.vector.tensor_tensor(mix_lo[:, m, k, :], (acc if m else work)[:, k, :],
                                            mix_hi[:, m, k, :], ALU.subtract).then_inc(mix_ready, 1)

            for i in (0, 1):
                dve.wait_ge(att_w_hi, i + 1)
                nc.vector.tensor_tensor(xT_lo[:, att_at[i], :, :], att_raw[i],
                                        xT_hi[:, att_at[i], :, :], ALU.subtract).then_inc(att_w_ready, 1)
            fw_slice(0)
            fw_slice(1)
            mix_split(0)
            fw_slice(2)
            fw_slice(3)
            norm_stats(0, 0, True)
            norm_stats(0, 1, True)

            normed2, hi_tiles, att_his = [0], [0], [0]

            def normalise(key):
                _, li, c, half = key
                dve.wait_ge(rstd_ready, 4 * li + c + 1)
                if LAYERS[li] != "T":
                    for j in range(2):
                        i = c * TT + 2 * half + j
                        nc.vector.tensor_scalar(normed_tile(c, half, j), halves(x[:, i, :]), meanvar[:, i, 0:1],
                                                rstd[:, i:i + 1], ALU.subtract, ALU.mult).then_inc(xn_ready, 1)
                    return
                if normed2[0]:
                    dve.wait_ge(y_added, 2 * normed2[0])
                    dve.wait_ge(xn_ready, 8 * li + 2 * normed2[0])
                for j in range(2):
                    i = c * TT + 2 * half + j
                    last = nc.vector.tensor_scalar(xn[j][:, :], x[:, i, :], meanvar[:, i, 0:1], rstd[:, i:i + 1],
                                                   ALU.subtract, ALU.mult)
                link(last)
                for j in range(2):
                    last = nc.vector.bn_stats(stats2[:, j, :], xn[j][:, :])
                link(last)
                for j in range(2):
                    last = nc.vector.bn_aggr(meanvar2[:, j, :], stats2[:, j, :])
                last.then_inc(stats2_ready, 1)
                normed2[0] += 1

            def transpose_pair(key):
                w = use[key]
                for j in range(2):
                    hi_tiles[0] += 1
                    dve.wait_ge(xT_hi_ready, hi_tiles[0])
                    ts = slice((2 * key[3] + j) * P, (2 * key[3] + j + 1) * P)
                    last = nc.vector.tensor_tensor(
                        xT_lo[:, key[2], :, ts],
                        work[:, w % 2 * 2 + j, :].rearrange("p (k t) -> p k t", k=KD),
                        xT_hi[:, key[2], :, ts], ALU.subtract)
                last.then_inc(pair_free, 1)

            def up(w, pair, n, h, li, blk):
                if LAYERS[li] == "S":
                    dve.wait_ge(hid_hi_ready, n + 1)
                    nc.vector.tensor_tensor(hid_lo[h][:, :], hid[h][:, :], hid_hi[h][:, :],
                                            ALU.subtract).then_inc(hid_lo_ready, 1)
                    dve.engine_nop().then_inc(pair_free, 1)
                    return
                dve.wait_ge(act_ready, n + 1)
                scale = up_s[:, blk:blk + 1] if LAYERS[li] == "B" else 1.0
                nc.vector.scalar_tensor_tensor(hid[h][:, :], work[:, 2 * pair + 1, :], scale, hid[h][:, :],
                                               ALU.mult, ALU.mult).then_inc(pair_free, 1)
                dve.wait_ge(hid_hi_ready, n + 1)
                nc.vector.tensor_tensor(hid_lo[h][:, :], hid[h][:, :], hid_hi[h][:, :],
                                        ALU.subtract).then_inc(hid_lo_ready, 1)

            def add_tiles(li, tile, c):
                for i in range(TT):
                    dve.wait_ge(acc_ready, tile + i + 1)
                    if LAYERS[li] == "B":
                        added = added_no(li, tile) - TT + i + 1
                        if not isinstance(added, int) or added > 0:
                            dve.wait_ge(x_added, added)
                        dve.wait_ge(half_ready, 1)
                        if li == LAST and isinstance(tile, int) and tile + TT == plan.tiles and i % 2:
                            link(nc.vector.tensor_tensor(scaled[:, i, :], acc[:, i, :], half_down_s[:, :],
                                                         ALU.mult))
                            at = c * TT + i
                            nc.vector.tensor_tensor(x[:, at, :], x[:, at, :], scaled[:, i, :],
                                                    ALU.add).then_inc(last_added, 1)
                            continue
                        nc.vector.tensor_tensor(scaled[:, i, :], acc[:, i, :], half_down_s[:, :],
                                                ALU.mult).then_inc(acc_free, 1)
                        continue
                    nc.vector.tensor_tensor(x[:, c * TT + i, :], acc[:, i, :], x[:, c * TT + i, :],
                                            ALU.add).then_inc(acc_free, 1)

            def split_part(li, g, part, no):
                size, buf = SIZES[LAYERS[li]][g], group_buffer(li, g)
                dve.wait_ge(w_hi_ready, no)
                nc.vector.tensor_tensor(w_lo[buf][:, part, 0:size * D], raw[:, part, 0:size * D],
                                        w_hi[buf][:, part, 0:size * D], ALU.subtract).then_inc(w_ready, 1)

            def finish_chunk(li, g, c):
                if li < LAST and g == len(SIZES[LAYERS[li]]) - 1:
                    if LAYERS[li] == "B":
                        dve.wait_ge(x_added, added_no(li, tile_no[li, g, c]) + TT)
                    else:
                        dve.wait_ge(acc_free, tile_no[li, g, c] + TT)
                    norm_stats(li + 1, c)

            def split_next(li, g, c0, c, b, dp):
                if b == 0 and following(li, g) and part_split(li, g, c0) is not None:
                    ln, gn = following(li, g)
                    part = c if part_split(li, g, c0) == c0 else c - 1
                    if LAYERS[ln] == "S":
                        split_part(ln, gn, part, parts_no[ln, gn] - 1 + part // 2)
                    else:
                        split_part(ln, gn, part, (parts_no[ln, gn] - 2 + dp) + part)

            def step(li, g, c0, c, d=0, dt=0, dp=0):
                kind = LAYERS[li]
                for b in range(SIZES[kind][g]):
                    w, n = use[li, g, c0, b], block_no[li, g, c0, b]
                    up(w + d, w % 2, n + d, n % 2, li, sum(SIZES[kind][:g]) + b)
                    split_first = SIZES[kind][g] == 1
                    if split_first:
                        split_next(li, g, c0, c, b, dp)
                    if b == 0 and c0:
                        add_tiles(li, tile_no[li, g, c0] - TT + dt, c - 1)
                    elif b == 0 and previous(li, g):
                        add_tiles(previous(li, g)[0], tile_no[li, g, c0] - TT + dt, CH - 1)
                    if b and isinstance(c, int):
                        if c0:
                            if LAYERS[min(li + 1, LAST)] != "T" or c0 > 1:
                                finish_chunk(li, g, c0 - 1)
                        elif g == 0 and previous(li, g):
                            finish_chunk(*previous(li, g), CH - 1)
                    if not split_first:
                        split_next(li, g, c0, c, b, dp)
                    if (li, g, c0, b) in plan.after:
                        key = plan.after[li, g, c0, b]
                        if key[3] == 0 and LAYERS[key[1]] == "T":
                            normalise(key[:3] + (1,))
                        transpose_pair(key)
                    if b == 0 and c0 == 1 and isinstance(c, int) and LAYERS[min(li + 1, LAST)] == "T":
                        finish_chunk(li, g, c0 - 1)
                if isinstance(c, int) and c and g == len(SIZES[kind]) - 1 and li < LAST:
                    normalise(("x", li + 1, c - 1, 0))
                    if LAYERS[li + 1] != "T":
                        normalise(("x", li + 1, c - 1, 1))
                if g == 0 and isinstance(c, int) and c == 0 and li:
                    normalise(("x", li, CH - 1, 0))
                    normalise(("x", li, CH - 1, 1))
                if g == 0 and li == 0 and c < 2:
                    normalise(("x", li, c + 2, 0))
                    normalise(("x", li, c + 2, 1))
                    if c == 0:
                        norm_stats(0, 3, True)

            def group(li, g, d=0, dt=0, dp=0):
                step(li, g, 0, 0, d, dt, dp)
                G = len(SIZES[LAYERS[li]])
                if g in (0, G - 1) or LAYERS[li] == "B":
                    for c in range(1, CH):
                        step(li, g, c, c, d, dt, dp)
                else:
                    with dve.Fori(0, CH - 2) as e:
                        step(li, g, 1, e + 1, e * 2 + d, e * TT + dt, dp)
                    step(li, g, CH - 1, CH - 1, d, dt, dp)

            def pair_lo(key, dst_hi, dst_lo):
                w = use[key]
                for i in range(2):
                    att_his[0] += 1
                    dve.wait_ge(att_hi_ready, att_his[0])
                    last = nc.vector.tensor_tensor(dst_lo[:, 2 * key[2] + i, :], work[:, w % 2 * 2 + i, :],
                                                   dst_hi[:, 2 * key[2] + i, :], ALU.subtract)
                last.then_inc(pair_free, 1)

            def maxima(c, i):
                dve.wait_ge(score_ready, TT * c + i + 1)
                n = (i + 1) * P
                link(nc.vector.tensor_tensor(acc[:, i, n - P:n], acc[:, i, n - P:n], causal[:, :], ALU.add))
                link(nc.vector.reduce_max(rowmax[:, i:i + 1], acc[:, i, 0:n], AX.X))
                nc.vector.tensor_scalar(negmax[:, i:i + 1], rowmax[:, i:i + 1], -SCORE_SCALE, None,
                                        ALU.mult).then_inc(max_ready, 1)

            def p_lo(c, i):
                att_his[0] += 1
                dve.wait_ge(att_hi_ready, att_his[0])
                n = (i + 1) * P
                nc.vector.tensor_tensor(hid_lo[i % 2][:, 0:n], acc[:, i, 0:n],
                                        hid_hi[i % 2][:, 0:n], ALU.subtract).then_inc(p_ready, 1)

            def attended(c, i):
                link(nc.vector.reciprocal(rowinv[:, i:i + 1], rowsum[:, i:i + 1]))
                dve.wait_ge(acc_ready, tile_no[1, c] + i + 1)
                dve.wait_ge(y_added, TT * c + i + 1)
                nc.vector.scalar_tensor_tensor(x[:, c * TT + i, :], acc[:, i, :], rowinv[:, i:i + 1],
                                               x[:, c * TT + i, :], ALU.mult, ALU.add).then_inc(acc_free, 1)

            def attention(li):
                pair_lo(("q", 0, 0), qT_hi, qT_lo)
                lp, gp = li - 1, len(SIZES[LAYERS[li - 1]]) - 1
                add_tiles(lp, tile_no[lp, gp, CH - 1], CH - 1)
                pair_lo(("q", 0, 1), qT_hi, qT_lo)
                finish_chunk(lp, gp, CH - 1)
                normalise(("x", 1, 2, 1))
                for c in range(CH):
                    more = c + 1 < CH
                    first = ("x", 1, c + 2) if c < 2 else ("x", 2, c - 1)
                    pair_lo(("v", c, 0), v_hi, v_lo)
                    for i in range(TT):
                        maxima(c, i)
                    if c:
                        normalise(first + (0,))
                    p_lo(c, 0)
                    p_lo(c, 1)
                    if c:
                        normalise(first + (1,))
                    pair_lo(("v", c, 1), v_hi, v_lo)
                    attended(c, 0)
                    attended(c, 1)
                    p_lo(c, 2)
                    transpose_pair(first + (0,))
                    if more:
                        pair_lo(("q", c + 1, 0), qT_hi, qT_lo)
                    p_lo(c, 3)
                    transpose_pair(first + (1,))
                    attended(c, 2)
                    if c == 1:
                        normalise(("x", 2, 0, 0))
                        normalise(("x", 2, 0, 1))
                    if more:
                        pair_lo(("q", c + 1, 1), qT_hi, qT_lo)
                    else:
                        for part in range(3):
                            split_part(li + 1, 0, part, parts_no[li + 1, 0] - 2 + part)
                    if c == 1:
                        transpose_pair(("x", 2, 0, 0))
                        transpose_pair(("x", 2, 0, 1))
                    attended(c, 3)
                    dve.wait_ge(acc_free, tile_no[li, c] + TT)
                    norm_stats(li + 1, c)

            for part in (0, 1):
                split_part(0, 0, part, part + 1)
            normalise(("x", 0, 0, 0))
            normalise(("x", 0, 0, 1))
            mix_split(1)
            transpose_pair(("x", 0, 0, 0))
            transpose_pair(("x", 0, 0, 1))
            normalise(("x", 0, 1, 0))
            normalise(("x", 0, 1, 1))
            split_part(0, 0, 2, 3)
            norm_stats(0, 2, True)
            for li, kind in enumerate(LAYERS):
                G = len(SIZES[kind])
                if kind == "T":
                    attention(li)
                elif kind == "A":
                    group(li, 0)
                    with dve.Fori(0, (G - 2) // 2) as o:
                        group(li, 1, o * 16, o * 32, o * 6)
                        group(li, 2, o * 16, o * 32, o * 6)
                    group(li, G - 1)
                else:
                    for g in range(G):
                        group(li, g)
            add_tiles(LAST, tile_no[LAST, len(SIZES["B"]) - 1, CH - 1], CH - 1)


def _counts():
    raw, n = {}, -32
    for li, kind in enumerate(LAYERS):
        for g in range(len(SIZES[kind])):
            n += 32 if kind == "S" else 48
            raw[li, g] = n
    return raw


raw_count = _counts()


def kernel(**inputs):
    import concourse.bacc as bacc
    from concourse.bass_utils import run_bass_kernel_spmd

    a = {k: np.asarray(v) for k, v in inputs.items()}

    def up_blocks(w):
        h = w.shape[0]
        return w.reshape(h // P, P, KD, P).transpose(0, 3, 2, 1).reshape(h // P, P, KD * P)

    def down_blocks(w):
        return w.T.reshape(w.shape[1] // P, P, D)

    def rows(w):
        return w.reshape(KD, P, w.shape[1]).transpose(1, 0, 2)

    def column(v):
        return v.reshape(-1, P).T

    hadamard = np.array([[1.0]], np.float32)
    while len(hadamard) < P:
        hadamard = np.block([[hadamard, hadamard], [hadamard, -hadamard]])
    causal = np.where(np.arange(P)[None, :] <= np.arange(P)[:, None], 0.0, MASKED).astype(np.float32)
    qkv = a["L0_attn_qkv"]
    arrays = {
        "x": a["L0_attn_x"].reshape(CH * TT, P, D).transpose(1, 0, 2),
        "w1a": up_blocks(a["L0_ffn_W1"]),
        "w3a": up_blocks(a["L0_ffn_W3"]),
        "w2a": a["L0_ffn_W2"].reshape(4, P, HA // P, P).transpose(0, 3, 2, 1),
        "att_w": np.stack([rows(qkv[:, 0:D].T), rows(qkv[:, D:2 * D].T), rows(qkv[:, 2 * D:].T),
                           rows(a["L0_attn_o_proj"])]),
        "gate": up_blocks(a["L1_ffn_gate_w"]),
        "up": up_blocks(a["L1_ffn_up_w"]),
        "down": down_blocks(a["L1_ffn_down_w"]),
        "b": up_blocks(a["L1_attn_B"]),
        "c": down_blocks(a["L1_attn_C"]),
        "small": np.concatenate([column(a["L0_attn_gamma"]), column(a["L0_attn_beta"]),
                                 column(a["L1_attn_D"]),
                                 column(a["L1_ffn_gate_s"]), column(a["L1_ffn_up_s"])], axis=1),
        "down_s": np.broadcast_to(a["L1_ffn_down_s"][None, :], (P, D)),
        "ident": np.eye(P, dtype=np.float32),
        "hadamard": hadamard,
        "causal": causal,
    }
    arrays = {k: np.ascontiguousarray(v) for k, v in arrays.items()}
    nc = bacc.Bacc("TRN2", target_bir_lowering=False, num_devices=1)
    t = {k: nc.dram_tensor(f"in_{k}", v.shape, F32, kind="ExternalInput").ap() for k, v in arrays.items()}
    t["out"] = nc.dram_tensor("out_x", (P, CH * TT, D), F32, kind="ExternalOutput").ap()
    build(nc, t)
    r = run_bass_kernel_spmd(nc, [{f"in_{k}": v for k, v in arrays.items()}], core_ids=[0])
    out = r.results[0]["out_x"]
    return np.ascontiguousarray(out.transpose(1, 0, 2).reshape(CH, TOK, D))
```
